# Optimizing a Trainium2 kernel written in Bass

```python
import numpy as np
import jax
import jax.numpy as jnp

def _softmax(x, axis=-1):
    return jax.nn.softmax(x, axis=axis)

def _gelu(x):
    return jax.nn.gelu(x, approximate=True)

def _silu(x):
    return jax.nn.silu(x)

def _sigmoid(x):
    return jax.nn.sigmoid(x)

def _layernorm(x, axis=-1, eps=1e-05):
    m = jnp.mean(x, axis=axis, keepdims=True)
    v = jnp.var(x, axis=axis, keepdims=True)
    return (x - m) / jnp.sqrt(v + eps)

def _scatter_add(tgt, idx, src, axis=0):
    return tgt.at[idx].add(src)

def _segment_sum(src, seg, n):
    return jax.ops.segment_sum(src, seg, n)
kernel_name = 'mk_adj_ffn_d1_adj_r2_e119fa'

def setup_inputs(seed: int=0):
    np.random.seed(seed)
    _w = jnp.asarray

    def _rec_inputs():
        import jax
        import jax.numpy as jnp
        _gk = jax.random.key(seed)
        x = -0.0002928 + 1 * jax.random.normal(jax.random.fold_in(_gk, 1), (32, 256, 128), jnp.float32)
        _a = jax.random.bernoulli(jax.random.fold_in(_gk, 2), 0.015625, (32, 256, 256))
        _a = jnp.logical_or(_a, jnp.swapaxes(_a, -1, -2))
        _a = jnp.logical_or(_a, jnp.eye(256, dtype=bool))
        _af = _a.astype(jnp.float32)
        _af = _af * jax.random.uniform(jax.random.fold_in(_gk, 3), (32, 256, 256), jnp.float32, 0.05, 1)
        adj = _af
        return (x, adj)
    x, adj = _rec_inputs()

    def _L0_gnn_setup():
        import jax, jax.numpy as jnp
        import numpy as np
        B, N, D, H = (8, 1024, 128, 512)
        RMS_EPS = 1e-06

        def _rmsnorm(h, w, eps=RMS_EPS):
            var = jnp.mean(jnp.square(h), axis=-1, keepdims=True)
            return h * jax.lax.rsqrt(var + eps) * w
        key = jax.random.key(seed)
        ks = jax.random.split(key, 5)
        x = jax.random.normal(ks[0], (B, N, D), dtype=jnp.float32)
        adjacency = jax.random.uniform(ks[1], (B, N, N), dtype=jnp.float32)
        epsilon = jnp.zeros((), dtype=jnp.float32)
        W1 = jax.random.normal(ks[2], (D, H), dtype=jnp.float32) * (1.0 / np.sqrt(D))
        b1 = jnp.zeros((H,), dtype=jnp.float32)
        rms_weight = jnp.ones((H,), dtype=jnp.float32)
        W2 = jax.random.normal(ks[3], (H, D), dtype=jnp.float32) * (1.0 / np.sqrt(H))
        b2 = jnp.zeros((D,), dtype=jnp.float32)
        return {'x': x, 'adjacency': adjacency, 'epsilon': epsilon, 'W1': W1, 'b1': b1, 'rms_weight': rms_weight, 'W2': W2, 'b2': b2}
    _L0_gnn_all = _L0_gnn_setup()
    _L0_gnn_in = {k: v for k, v in _L0_gnn_all.items() if k in ('epsilon', 'W1', 'b1', 'rms_weight', 'W2', 'b2')}
    del _L0_gnn_all

    def _L0_ffn_setup():
        import jax, jax.numpy as jnp
        import numpy as np
        E = 8
        K = 2
        D = 128
        H = 256
        DOUT = 128
        EPS = 1e-05
        key = jax.random.key(seed)
        ks = jax.random.split(key, 9)
        s = 0.02
        return {'x': jax.random.normal(ks[0], (4, 4096, D), jnp.float32), 'gamma': 1.0 + 0.05 * jax.random.normal(ks[1], (D,), jnp.float32), 'beta': 0.05 * jax.random.normal(ks[2], (D,), jnp.float32), 'Wr': 0.01 * jax.random.normal(ks[3], (D, E), jnp.float32), 'br': jnp.zeros((E,), jnp.float32), 'W1': s * jax.random.normal(ks[4], (E, D, H), jnp.float32), 'b1': s * jax.random.normal(ks[5], (E, H), jnp.float32), 'W2': s * jax.random.normal(ks[6], (E, H, DOUT), jnp.float32), 'b2': s * jax.random.normal(ks[7], (E, DOUT), jnp.float32)}
    _L0_ffn_all = _L0_ffn_setup()
    _L0_ffn_in = {k: v for k, v in _L0_ffn_all.items() if k in ('gamma', 'beta', 'Wr', 'br', 'W1', 'b1', 'W2', 'b2')}
    del _L0_ffn_all
    return {'x': x, 'adj': adj, 'L0_gnn_epsilon': _L0_gnn_in['epsilon'], 'L0_gnn_W1': _L0_gnn_in['W1'], 'L0_gnn_b1': _L0_gnn_in['b1'], 'L0_gnn_rms_weight': _L0_gnn_in['rms_weight'], 'L0_gnn_W2': _L0_gnn_in['W2'], 'L0_gnn_b2': _L0_gnn_in['b2'], 'L0_ffn_gamma': _L0_ffn_in['gamma'], 'L0_ffn_beta': _L0_ffn_in['beta'], 'L0_ffn_Wr': _L0_ffn_in['Wr'], 'L0_ffn_br': _L0_ffn_in['br'], 'L0_ffn_W1': _L0_ffn_in['W1'], 'L0_ffn_b1': _L0_ffn_in['b1'], 'L0_ffn_W2': _L0_ffn_in['W2'], 'L0_ffn_b2': _L0_ffn_in['b2']}

def reference(x, adj, L0_gnn_epsilon, L0_gnn_W1, L0_gnn_b1, L0_gnn_rms_weight, L0_gnn_W2, L0_gnn_b2, L0_ffn_gamma, L0_ffn_beta, L0_ffn_Wr, L0_ffn_br, L0_ffn_W1, L0_ffn_b1, L0_ffn_W2, L0_ffn_b2):
    import jax
    import jax.numpy as jnp

    def _L0_gnn_ref(x, adjacency, epsilon, W1, b1, rms_weight, W2, b2):
        import jax, jax.numpy as jnp
        import numpy as np
        B, N, D, H = (8, 1024, 128, 512)
        RMS_EPS = 1e-06

        def _rmsnorm(h, w, eps=RMS_EPS):
            var = jnp.mean(jnp.square(h), axis=-1, keepdims=True)
            return h * jax.lax.rsqrt(var + eps) * w
        neighbor_sum = jnp.einsum('bnm,bmd->bnd', adjacency, x)
        agg = epsilon * x + neighbor_sum
        h = jnp.einsum('bnd,dh->bnh', agg, W1) + b1
        h = jax.nn.silu(_rmsnorm(h, rms_weight))
        out = jnp.einsum('bnh,hd->bnd', h, W2) + b2
        return out

    def _L0_ffn_ref(x, gamma, beta, Wr, br, W1, b1, W2, b2):
        import jax, jax.numpy as jnp
        import numpy as np
        E = 8
        K = 2
        D = 128
        H = 256
        DOUT = 128
        EPS = 1e-05
        mu = jnp.mean(x, axis=-1, keepdims=True)
        var = jnp.mean(jnp.square(x - mu), axis=-1, keepdims=True)
        xn = (x - mu) * jax.lax.rsqrt(var + EPS) * gamma + beta
        logits = jnp.einsum('bsd,de->bse', xn, Wr) + br
        top_vals, top_idx = jax.lax.top_k(logits, K)
        w = jax.nn.softmax(top_vals, axis=-1)
        w_full = jnp.einsum('bsk,bske->bse', w, jax.nn.one_hot(top_idx, E, dtype=w.dtype))
        y = jnp.zeros(x.shape[:-1] + (DOUT,), x.dtype)
        for e in range(E):
            h = jax.nn.gelu(jnp.einsum('bsd,dh->bsh', xn, W1[e]) + b1[e], approximate=False)
            y_e = jnp.einsum('bsh,hd->bsd', h, W2[e]) + b2[e]
            y = y + y_e * w_full[..., e, None]
        return y
    x = x + _L0_gnn_ref(_layernorm(x, axis=-1), adj, L0_gnn_epsilon, L0_gnn_W1, L0_gnn_b1, L0_gnn_rms_weight, L0_gnn_W2, L0_gnn_b2)
    x = x + _L0_ffn_ref(_layernorm(x, axis=-1), L0_ffn_gamma, L0_ffn_beta, L0_ffn_Wr, L0_ffn_br, L0_ffn_W1, L0_ffn_b1, L0_ffn_W2, L0_ffn_b2)
    return x

_drawn_inputs = setup_inputs


def setup_inputs(seed=0):
    import zlib

    import numpy as np

    out = dict(_drawn_inputs(seed))
    spreads = {'L0_gnn_b1': (0.0, 0.1),
     'L0_gnn_rms_weight': (1.0, 0.2),
     'L0_gnn_b2': (0.0, 0.1),
     'L0_ffn_br': (0.0, 0.292)}
    factors = {'L0_ffn_gamma': 8.0,
     'L0_ffn_beta': 8.0,
     'L0_ffn_Wr': 3.772,
     'L0_ffn_b1': 8.0,
     'L0_ffn_b2': 4.877}
    for name, (base, spread) in spreads.items():
        noise = np.random.default_rng([zlib.crc32(name.encode()), seed]).standard_normal(out[name].shape)
        drawn = base * np.exp(spread * noise) if base else spread * noise
        out[name] = jnp.asarray(drawn.astype(out[name].dtype))
    for name, factor in factors.items():
        out[name] = (out[name] * factor).astype(out[name].dtype)
    return out
```

```python
from contextlib import ExitStack

import numpy as np

import concourse.bass as bass
from concourse import mybir

P = 128
D = 128
NTOK = 32 * 256
GT = 512
NG = NTOK // GT
TPG = GT // P
NODES = 256
H1 = 512
HC1 = H1 // P
E = 8
HE = 256
HCE = HE // P
UNITS = E * HCE
NQ = 4
GPQ = NG // NQ
TPQ = GPQ * TPG
LN_EPS = 1e-5
RMS_EPS = 1e-6

F32 = mybir.dt.float32
F32R = mybir.dt.float32r
ALU = mybir.AluOpType
ACT = mybir.ActivationFunctionType
AX = mybir.AxisListType

PEEL = 6
MAX_LAG = 5
LOOPS = (NG - PEEL) // 2


class Group:

    def __init__(self, pair, offset):
        self.index = pair * 2 + offset
        self.half = pair + offset // 2
        self.parity = offset % 2
        self.tokens = self.index * GT

    def after(self, n):
        return not isinstance(self.index, int) or self.index >= n


def steps(engine, step):
    def peeled(s):
        return lambda lag: Group(0, s - lag) if 0 <= s - lag < NG else None

    for s in range(PEEL):
        step(peeled(s))
    with engine.Fori(0, LOOPS) as pair:
        for k in range(2):
            step(lambda lag, k=k: Group(pair, PEEL + k - lag))
    for s in range(PEEL + 2 * LOOPS, NG + MAX_LAG):
        step(peeled(s))


def build(nc, x, x_t, adj_t, eps, gw1, gb1, rms_w, gw2, gb2, gamma, beta, wr, br, w1, b1, w2, b2,
          ident_in, descend_in, out_t):
    with ExitStack() as ctx:
        def sb(name, shape, dt=F32):
            return ctx.enter_context(nc.sbuf_tensor(name, shape, dt))

        def sem(name):
            return ctx.enter_context(nc.semaphore(name))

        x2t = sb("x2t", [P, NTOK])
        xg_hi = sb("xg_hi", [P, NTOK], F32R)
        xg_lo = sb("xg_lo", [P, NTOK], F32R)
        w1_hi = sb("w1_hi", [P, E * HE], F32R)
        w1_lo = sb("w1_lo", [P, E * HE], F32R)
        w2_hi = sb("w2_hi", [P, UNITS * D], F32R)
        w2_lo = sb("w2_lo", [P, UNITS * D], F32R)
        ident = sb("ident", [P, P])
        b1_col = sb("b1_col", [P, UNITS])
        b2_rows = sb("b2_rows", [E, D])
        logits = sb("logits", [P, NQ, TPQ * E])
        h_hi = sb("h_hi", [P, 4, GT], F32R)
        h_lo = sb("h_lo", [P, 4, GT], F32R)
        descend = sb("descend", [P, TPQ * E])
        eps_col = sb("eps_col", [P, 1])
        gamma_col = sb("gamma_col", [P, 1])
        beta_col = sb("beta_col", [P, 1])
        gb2_col = sb("gb2_col", [P, 1])
        br_col = sb("br_col", [E, 1])
        wr_sb = sb("wr_sb", [P, E])
        minus_half, ln_eps, rms_eps, one_and_eps, eps_squared = (
            sb(name, [P, TPG]) for name in ("minus_half", "ln_eps", "rms_eps", "one_and_eps", "eps_squared"))
        euler = sb("euler", [P, TPQ])
        bias_sel = sb("bias_sel", [P, P], F32R)
        bias_parts = sb("bias_parts", [P, H1], F32R)
        bn1 = sb("bn1", [P, TPG, 6])
        bn2 = sb("bn2", [P, TPG, 6])
        mv1 = sb("mv1", [P, 2, TPG, 2])
        mv2 = sb("mv2", [P, 2, TPG, 2])
        var1 = sb("var1", [P, TPG])
        var2 = sb("var2", [P, TPG])
        rstd1 = sb("rstd1", [P, 2, TPG])
        rstd2 = sb("rstd2", [P, 2, TPG])
        sumsq = sb("sumsq", [P, 2, TPG])
        meansq = sb("meansq", [P, TPG])
        rrms = sb("rrms", [P, 2, TPG])
        logit_rows = sb("logit_rows", [E, GT])

        AREA = 13440
        area = sb("area", [P, AREA])
        taken = [0]

        def part(*shape):
            n = int(np.prod(shape))
            view = area[:, taken[0]:taken[0] + n]
            taken[0] += n
            assert taken[0] <= AREA
            if len(shape) == 2:
                view = view.rearrange("p (a b) -> p a b", a=shape[0])
            if len(shape) == 3:
                view = view.rearrange("p (a b c) -> p a b c", a=shape[0], b=shape[1])
            return view

        x_tok = part(2, TPG, D)
        adj = part(2, TPG, NODES)
        x_feat = part(2, GT)
        xn1 = part(2, TPG, D)
        agg = part(2, GT)
        gw1_sb = part(H1)
        gw2_sb = part(HC1, D)
        rms_bc = part(H1)
        hidden = part(TPG, H1)
        hidden_t = part(HC1, GT)
        xn2 = part(TPG, D)
        xg = part(2, GT)
        eps_ident = part(P)
        w1_raw = x2t[:, NTOK - E * HE:]
        w2_raw = x2t[:, NTOK - 2 * E * HE:NTOK - E * HE]
        bias_raw = x2t[:, NTOK - 2 * E * HE - H1:NTOK - 2 * E * HE]
        bias_hi = x2t[:, NTOK - 2 * E * HE - 2 * H1:NTOK - 2 * E * HE - H1].bitcast(F32R)
        taken[0] = 0
        gate_bc = part(2, E, GT)
        act_out = part(4, GT)
        gate_rows = part(2, GT)[0:E]
        first = part(TPQ, E)
        second = part(TPQ, E)
        masked = part(TPQ, E)
        score = part(TPQ, E)
        gates = part(NQ, TPQ * E)
        gates_t = part(NQ, P)
        top1 = part(TPQ)
        top2 = part(TPQ)
        place = part(TPQ)
        apart = part(TPQ)
        power = part(TPQ)
        denom = part(TPQ)
        share1 = part(TPQ)
        share2 = part(TPQ)

        gates_dram = nc.dram_tensor("gates_dram", (E, NTOK), F32).ap()

        banks = ctx.enter_context(nc.psum_tensor("banks", [P, 8, GT], F32))
        agg_ps, hid_ps, hidt_ps, z_ps, tok_ps, feat_ps, lg_ps = (
            banks[:, 0], banks[:, 1:3], banks[:, 3], banks[:, 4], banks[:, 5], banks[:, 6], banks[:, 7])
        f_ps, y_ps, turn_ps = banks[:, 0:4], banks[:, 4:6], banks[:, 7]

        x_in = [sem(f"x_in{p}") for p in range(2)]
        adj_in = [sem(f"adj_in{p}") for p in range(2)]
        xf_in = [sem(f"xf_in{p}") for p in range(2)]
        consts_in = sem("consts_in")
        w1_in = sem("w1_in")
        w2_in = sem("w2_in")
        gate_bc_in = [sem(f"gate_bc_in{p}") for p in range(2)]
        gate_rows_in = [sem(f"gate_rows_in{p}") for p in range(2)]
        gates_stored = sem("gates_stored")
        out_stored = sem("out_stored")
        fills_done = sem("fills_done")
        pool_consts = sem("pool_consts")
        bias_ready = sem("bias_ready")
        prep_chain = sem("prep_chain")
        weights_split = sem("weights_split")
        bn1_done = sem("bn1_done")
        stats1_ready = sem("stats1_ready")
        var1_ready = sem("var1_ready")
        rstd1_ready = sem("rstd1_ready")
        xn1_ready = sem("xn1_ready")
        adj_ready = sem("adj_ready")
        agg_done = sem("agg_done")
        agg_copied = sem("agg_copied")
        hid_done = sem("hid_done")
        sumsq_ready = sem("sumsq_ready")
        meansq_ready = sem("meansq_ready")
        rrms_ready = sem("rrms_ready")
        normed = sem("normed")
        silu_done = sem("silu_done")
        hidt_turned = sem("hidt_turned")
        hidt_copied = sem("hidt_copied")
        z_done = sem("z_done")
        x2_ready = sem("x2_ready")
        x2_kept = sem("x2_kept")
        tok_turned = sem("tok_turned")
        bn2_done = sem("bn2_done")
        stats2_ready = sem("stats2_ready")
        var2_ready = sem("var2_ready")
        rstd2_ready = sem("rstd2_ready")
        xn2_ready = sem("xn2_ready")
        feat_turned = sem("feat_turned")
        xg_ready = sem("xg_ready")
        xg_hi_ready = sem("xg_hi_ready")
        xg_lo_ready = sem("xg_lo_ready")
        lg_done = sem("lg_done")
        lg_copied = sem("lg_copied")
        lg_turned = sem("lg_turned")
        logits_ready = sem("logits_ready")
        route_chain = sem("route_chain")
        apart_ready = sem("apart_ready")
        power_ready = sem("power_ready")
        gates_ready = sem("gates_ready")
        gates_turned = sem("gates_turned")
        gates_copied = sem("gates_copied")
        f_done = sem("f_done")
        gelu_done = sem("gelu_done")
        gated = sem("gated")
        hi_ready = sem("hi_ready")
        lo_ready = sem("lo_ready")
        g_done = sem("g_done")
        out_ready = sem("out_ready")

        x_view = x.rearrange("(g t p) d -> p g t d", p=P, t=TPG)
        adj_view = adj_t.rearrange("(g t p) n -> p g t n", p=P, t=TPG)
        small_loads = [
            (ident[:], ident_in), (eps_col[:], eps.partition_broadcast(P)),
            (gw1_sb, gw1), (rms_bc, rms_w.partition_broadcast(P)),
            (gw2_sb, gw2.rearrange("(c p) d -> p c d", p=P)),
            (gb2_col[:], gb2), (gamma_col[:], gamma), (beta_col[:], beta),
            (wr_sb[:], wr), (br_col[:], br), (descend[:], descend_in),
            (b1_col[:], b1), (b2_rows[:], b2),
            (bias_raw[0:1, :], gb1), (bias_raw[32:33, :], gb1),
        ]
        CONSTS = 16 * len(small_loads)

        block = ctx.enter_context(nc.Block())

        @block.sync
        def _(sp):
            def step(at):
                if g := at(0):
                    if g.after(2):
                        sp.wait_ge(xn1_ready, g.index - 1)
                    sp.dma_start(x_tok[:, g.parity], x_view[:, bass.ds(g.index, 1)].squeeze(1)
                                 ).then_inc(x_in[g.parity], 16)
                    if g.after(2):
                        sp.wait_ge(agg_done, g.index - 1)
                    sp.dma_start(adj[:, g.parity], adj_view[:, bass.ds(g.index, 1)].squeeze(1)
                                 ).then_inc(adj_in[g.parity], 16)
                if g := at(2):
                    if g.after(2):
                        sp.wait_ge(tok_turned, g.index - 1)
                        sp.wait_ge(x2_kept, g.index - 1)
                    sp.dma_start(x_feat[:, g.parity], x_t[:, bass.ds(g.tokens, GT)]
                                 ).then_inc(xf_in[g.parity], 16)

            steps(sp, step)

            def store_gates(q):
                sp.wait_ge(gates_copied, q + 1)
                sp.dma_start(gates_dram[:, q * TPQ * P:(q + 1) * TPQ * P].rearrange("e (t p) -> t e p", p=P),
                             gates_t[:, q]).then_inc(gates_stored, 16)
                sp.wait_ge(gates_stored, 16 * (q + 1))

            def load_gates(g):
                if g.after(2):
                    sp.wait_ge(gated, UNITS * (g.index - 1))
                    sp.wait_ge(g_done, UNITS * (g.index - 1))
                rows = gates_dram[:, bass.ds(g.tokens, GT)]
                sp.dma_start(gate_bc[:, g.parity], rows.partition_broadcast(P)
                             ).then_inc(gate_bc_in[g.parity], 16)
                sp.dma_start(gate_rows[:, g.parity], rows).then_inc(gate_rows_in[g.parity], 16)

            def store_out(g):
                sp.wait_ge(out_ready, g.index + 1)
                sp.dma_start(out_t[:, bass.ds(g.tokens, GT)], x2t[:, bass.ds(g.tokens, GT)]
                             ).then_inc(out_stored, 16)

            store_gates(0)
            for g in range(2):
                load_gates(Group(0, g))
            for q in range(1, NQ):
                store_gates(q)
            with sp.Fori(0, NG // 2 - 1) as pair:
                for k in range(2):
                    load_gates(Group(pair, 2 + k))
                    store_out(Group(pair, k))
            for g in range(NG - 2, NG):
                store_out(Group(0, g))
            sp.wait_ge(out_stored, 16 * NG)

        @block.gpsimd
        def _(pool):
            nc.gpsimd.memset(minus_half[:], -0.5)
            nc.gpsimd.memset(ln_eps[:], LN_EPS)
            nc.gpsimd.memset(rms_eps[:], RMS_EPS)
            nc.gpsimd.memset(one_and_eps[:], 1.0 + LN_EPS)
            nc.gpsimd.memset(eps_squared[:], LN_EPS * LN_EPS)
            nc.gpsimd.memset(euler[:], float(np.e)).then_inc(pool_consts, 1)
            pool.wait_ge(consts_in, CONSTS)
            nc.gpsimd.tensor_scalar(eps_ident, ident[:], eps_col[:, 0:1], None, ALU.mult
                                    ).then_inc(pool_consts, 1)
            pool.wait_ge(pool_consts, 2)

            def step(at):
                if g := at(0):
                    p = g.parity
                    pool.wait_ge(adj_in[p], 16 * (g.half + 1))
                    for c in range(2):
                        block_c = adj[:, p].rearrange("p (b c) n -> p b c n", c=2)[:, :, c, c * P:(c + 1) * P]
                        last = nc.gpsimd.tensor_tensor(block_c, block_c,
                                                       eps_ident.unsqueeze(1).to_broadcast([P, 2, P]), ALU.add)
                    last.then_inc(adj_ready, 1)
                for t in range(TPG):
                    if g := at(2):
                        pool.wait_ge(sumsq_ready, TPG * g.index + t + 1)
                        nc.gpsimd.tensor_tensor(meansq[:, t:t + 1], sumsq[:, g.parity, t:t + 1], rms_eps[:, 0:1],
                                                ALU.add).then_inc(meansq_ready, 1)
                        pool.wait_ge(meansq_ready, TPG * g.index + t + 1)
                        nc.gpsimd.tensor_tensor(rrms[:, g.parity, t:t + 1], meansq[:, t:t + 1],
                                                minus_half[:, 0:1], ALU.pow).then_inc(rrms_ready, 1)
                    if t == 0 and (g := at(0)):
                        pool.wait_ge(stats1_ready, g.index + 1)
                        nc.gpsimd.tensor_tensor(var1[:], mv1[:, g.parity, :, 1], ln_eps[:], ALU.add).then_inc(var1_ready, 1)
                        pool.wait_ge(var1_ready, g.index + 1)
                        nc.gpsimd.tensor_tensor(rstd1[:, g.parity], var1[:], minus_half[:], ALU.pow
                                                ).then_inc(rstd1_ready, 1)
                if g := at(4):
                    pool.wait_ge(stats2_ready, g.index + 1)
                    nc.gpsimd.tensor_tensor(var2[:], mv2[:, g.parity, :, 1], one_and_eps[:], ALU.mult
                                            ).then_inc(var2_ready, 1)
                    pool.wait_ge(var2_ready, 2 * g.index + 1)
                    nc.gpsimd.tensor_tensor(var2[:], var2[:], eps_squared[:], ALU.add
                                            ).then_inc(var2_ready, 1)
                    pool.wait_ge(var2_ready, 2 * g.index + 2)
                    nc.gpsimd.tensor_tensor(rstd2[:, g.parity], var2[:], minus_half[:], ALU.pow
                                            ).then_inc(rstd2_ready, 1)

            steps(pool, step)
            for q in range(NQ):
                pool.wait_ge(apart_ready, q + 1)
                nc.gpsimd.tensor_tensor(power, euler[:], apart, ALU.pow).then_inc(power_ready, 1)

        @block.tensor
        def _(pe):
            def aggregate(g):
                pe.wait_ge(xn1_ready, g.index + 1)
                pe.wait_ge(adj_ready, g.index + 1)
                if g.after(1):
                    pe.wait_ge(agg_copied, g.index)
                for b in range(2):
                    for c in range(2):
                        last = pe.matmul(agg_ps[:, b * NODES:(b + 1) * NODES], xn1[:, g.parity, 2 * b + c],
                                         adj[:, g.parity, 2 * b + c], start=(c == 0), stop=(c == 1))
                last.then_inc(agg_done, 1)

            def widen(g, t):
                if t == 0:
                    pe.wait_ge(agg_copied, g.index + 1)
                    if not g.after(1):
                        pe.wait_ge(bias_ready, 1)
                if t >= 2 or g.after(1):
                    pe.wait_ge(normed, TPG * g.index + t - 1)
                pe.matmul(hid_ps[:, t % 2], agg[:, g.parity, t * P:(t + 1) * P], gw1_sb, start=True, stop=False)
                pe.matmul(hid_ps[:, t % 2], bias_sel[:], bias_parts[:], start=False, stop=True
                          ).then_inc(hid_done, 1)

            def turn_hidden(g, t):
                pe.wait_ge(silu_done, TPG * g.index + t + 1)
                if t >= 1 or g.after(1):
                    pe.wait_ge(hidt_copied, TPG * g.index + t)
                for c in range(HC1):
                    last = pe.transpose(hidt_ps[:, c * P:(c + 1) * P], hidden[:, t, c * P:(c + 1) * P], ident[:])
                last.then_inc(hidt_turned, 1)

            def narrow(g):
                pe.wait_ge(hidt_copied, TPG * (g.index + 1))
                if g.after(1):
                    pe.wait_ge(x2_ready, g.index)
                for c in range(HC1):
                    last = pe.matmul(z_ps, gw2_sb[:, c], hidden_t[:, c], start=(c == 0), stop=(c == HC1 - 1))
                last.then_inc(z_done, 1)

            def turn_to_tokens(g):
                pe.wait_ge(x2_ready, g.index + 1)
                if g.after(1):
                    pe.wait_ge(xn2_ready, g.index)
                for t in range(TPG):
                    last = pe.transpose(tok_ps[:, t * P:(t + 1) * P], x_feat[:, g.parity, t * P:(t + 1) * P],
                                        ident[:])
                last.then_inc(tok_turned, 1)

            def turn_to_features(g):
                pe.wait_ge(xn2_ready, g.index + 1)
                if g.after(1):
                    pe.wait_ge(xg_ready, g.index)
                for t in range(TPG):
                    last = pe.transpose(feat_ps[:, t * P:(t + 1) * P], xn2[:, t], ident[:])
                last.then_inc(feat_turned, 1)

            def router(g):
                pe.wait_ge(xg_ready, g.index + 1)
                if g.after(1):
                    pe.wait_ge(logits_ready, g.index)
                pe.matmul(lg_ps[0:E, :], wr_sb[:], xg[:, g.parity], start=True, stop=True).then_inc(lg_done, 1)

            def turn_logits(g):
                for t in range(TPG):
                    last = pe.transpose(lg_ps[:, t * E:(t + 1) * E], logit_rows[:, t * P:(t + 1) * P],
                                        ident[0:E, 0:E])
                last.then_inc(lg_turned, 1)

            def step(at):
                if g := at(1):
                    aggregate(g)
                for t in range(TPG):
                    if g := at(3):
                        turn_hidden(g, t)
                    if g := at(2):
                        widen(g, t)
                    if t == 1 and (g := at(4)):
                        turn_to_tokens(g)
                    if t == 2 and (g := at(5)):
                        router(g)
                if g := at(3):
                    narrow(g)
                if g := at(5):
                    pe.wait_ge(lg_copied, g.index + 1)
                if g := at(4):
                    turn_to_features(g)
                if g := at(5):
                    turn_logits(g)

            pe.wait_ge(consts_in, CONSTS)
            steps(pe, step)

            def expert_in(g, u):
                if u >= 4 or g.after(1):
                    pe.wait_ge(gelu_done, UNITS * g.index + u - 3)
                hi, lo = (w[:, u * P:(u + 1) * P] for w in (w1_hi, w1_lo))
                x_hi, x_lo = (v[:, bass.ds(g.tokens, GT)] for v in (xg_hi, xg_lo))
                pe.matmul(f_ps[:, u % 4], lo, x_hi, start=True, stop=False)
                pe.matmul(f_ps[:, u % 4], hi, x_lo, start=False, stop=False)
                pe.matmul(f_ps[:, u % 4], hi, x_hi, start=False, stop=True).then_inc(f_done, 1)

            def expert_out(g, u):
                y = y_ps[:, g.parity]
                if u == 0:
                    if g.after(2):
                        pe.wait_ge(out_ready, g.index - 1)
                    pe.wait_ge(gate_rows_in[g.parity], 16 * (g.half + 1))
                    pe.matmul(y, b2_rows[:], gate_rows[:, g.parity], start=True, stop=False)
                pe.wait_ge(hi_ready, UNITS * g.index + u + 1)
                hi, lo = (w[:, u * P:(u + 1) * P] for w in (w2_hi, w2_lo))
                pe.matmul(y, lo, h_hi[:, u % 4], start=False, stop=False)
                pe.matmul(y, hi, h_hi[:, u % 4], start=False, stop=False)
                pe.wait_ge(lo_ready, UNITS * g.index + u + 1)
                last = pe.matmul(y, hi, h_lo[:, u % 4], start=False, stop=(u == UNITS - 1))
                last.then_inc(g_done, 1)

            def turn_gates(q):
                pe.wait_ge(gates_ready, q + 1)
                if q >= 1:
                    pe.wait_ge(gates_copied, q)
                pe.transpose(turn_ps[:, q * P:(q + 1) * P], gates[:, q], ident[:]).then_inc(gates_turned, 1)

            BEHIND = 3
            pe.wait_ge(agg_copied, NG)
            pe.wait_ge(normed, TPG * NG)
            pe.wait_ge(hidt_copied, TPG * NG)
            pe.wait_ge(x2_ready, NG)
            pe.wait_ge(xn2_ready, NG)
            pe.wait_ge(logits_ready, NG)
            pe.wait_ge(weights_split, 2)
            pe.wait_ge(xg_lo_ready, NG)

            def group_units(g, before):
                for u in range(UNITS):
                    expert_in(g, u)
                    if u >= BEHIND:
                        expert_out(g, u - BEHIND)
                    elif before:
                        expert_out(before, UNITS + u - BEHIND)

            g0 = Group(0, 0)
            for u in range(UNITS):
                expert_in(g0, u)
                if u == BEHIND - 1:
                    for q in range(NQ):
                        turn_gates(q)
                if u >= BEHIND:
                    expert_out(g0, u - BEHIND)
            group_units(Group(0, 1), g0)
            with pe.Fori(0, NG // 2 - 1) as pair:
                for k in range(2):
                    group_units(Group(pair, 2 + k), Group(pair, 1 + k))
            g_last = Group(0, NG - 1)
            for u in range(UNITS - BEHIND, UNITS):
                expert_out(g_last, u)

        @block.scalar
        def _(act):
            for dst, src in small_loads:
                act.dma_start(dst, src).then_inc(consts_in, 16)
            act.dma_start(w1_raw.rearrange("p (e h) -> p e h", e=E),
                          w1.rearrange("e d h -> d e h")).then_inc(w1_in, 16)
            act.dma_start(w2_raw.rearrange("p (u d) -> p u d", u=UNITS),
                          w2.rearrange("e (c p) d -> p (e c) d", p=P)).then_inc(w2_in, 16)

            def step(at):
                if g := at(1):
                    act.wait_ge(agg_done, g.index + 1)
                    if g.after(2):
                        act.wait_ge(hid_done, TPG * (g.index - 1))
                    nc.scalar.activation(agg[:, g.parity], agg_ps, ACT.Copy).then_inc(agg_copied, 1)
                for t in range(TPG):
                    if g := at(3):
                        act.wait_ge(hidt_turned, TPG * g.index + t + 1)
                        if t == 0 and g.after(1):
                            act.wait_ge(z_done, g.index)
                        nc.scalar.activation(hidden_t[:, :, t * P:(t + 1) * P],
                                             hidt_ps.rearrange("p (c k) -> p c k", c=HC1), ACT.Copy
                                             ).then_inc(hidt_copied, 1)
                    if g := at(2):
                        act.wait_ge(hid_done, TPG * g.index + t + 1)
                        nc.scalar.activation(hidden[:, t], hid_ps[:, t % 2], ACT.Square, scale=H1 ** -0.5,
                                             accum_out=sumsq[:, g.parity, t:t + 1]).then_inc(sumsq_ready, 1)
                        if t >= 1:
                            silu(g, t - 1)
                    if t == 3 and (g := at(5)):
                        act.wait_ge(lg_done, g.index + 1)
                        nc.scalar.activation(logit_rows[:], lg_ps[0:E, :], ACT.Identity, bias=br_col[:, 0:1]
                                             ).then_inc(lg_copied, 1)
                if g := at(2):
                    silu(g, TPG - 1)
                if g := at(5):
                    act.wait_ge(lg_turned, g.index + 1)
                    nc.scalar.activation(logits[:].rearrange("p q n -> p (q n)")[:, bass.ds(g.index * (TPG * E), TPG * E)],
                                         lg_ps[:, 0:TPG * E], ACT.Copy).then_inc(logits_ready, 1)

            def silu(g, t):
                act.wait_ge(normed, TPG * g.index + t + 1)
                nc.scalar.activation(hidden[:, t], hidden[:, t], ACT.Silu).then_inc(silu_done, 1)

            act.wait_ge(consts_in, CONSTS)
            steps(act, step)

            def gelu(g, u):
                act.wait_ge(f_done, UNITS * g.index + u + 1)
                if u >= 4 or g.after(1):
                    act.wait_ge(lo_ready, UNITS * g.index + u - 3)
                nc.scalar.activation(act_out[:, u % 4], f_ps[:, u % 4], ACT.Gelu, bias=b1_col[:, u:u + 1]
                                     ).then_inc(gelu_done, 1)

            def high_part(g, u):
                act.wait_ge(gated, UNITS * g.index + u + 1)
                if u >= 4 or g.after(1):
                    act.wait_ge(g_done, UNITS * g.index + u - 3)
                nc.scalar.activation(h_hi[:, u % 4], act_out[:, u % 4], ACT.Copy).then_inc(hi_ready, 1)

            EARLY = 3
            g0 = Group(0, 0)
            for u in range(EARLY):
                gelu(g0, u)
            for q in range(NQ):
                act.wait_ge(gates_turned, q + 1)
                nc.scalar.activation(gates_t[:, q], turn_ps[:, q * P:(q + 1) * P], ACT.Copy
                                     ).then_inc(gates_copied, 1)
            for u in range(EARLY - 1):
                high_part(g0, u)
            for u in range(EARLY, UNITS):
                gelu(g0, u)
                high_part(g0, u - 1)

            def group_units(g, before):
                for u in range(UNITS):
                    gelu(g, u)
                    if u >= 1:
                        high_part(g, u - 1)
                    else:
                        high_part(before, UNITS - 1)

            group_units(Group(0, 1), g0)
            with act.Fori(0, NG // 2 - 1) as pair:
                for k in range(2):
                    group_units(Group(pair, 2 + k), Group(pair, 1 + k))
            high_part(Group(0, NG - 1), UNITS - 1)

        @block.vector
        def _(dve):
            def prep_bias():
                nc.vector.memset(bias_sel[:].bitcast(F32), 0.0)
                nc.vector.memset(bias_parts[:].bitcast(F32), 0.0).then_inc(fills_done, 1)
                dve.wait_ge(fills_done, 1)
                for r in (0, 32):
                    nc.vector.memset(bias_sel[r:r + 1, :].bitcast(F32), 1.0)
                dve.wait_ge(consts_in, CONSTS)
                nc.vector.tensor_copy(bias_parts[0:1, :], bias_raw[0:1, :])
                nc.vector.tensor_copy(bias_hi[32:33, :], bias_raw[32:33, :]).then_inc(fills_done, 1)
                dve.wait_ge(fills_done, 2)
                nc.vector.tensor_tensor(bias_parts[32:33, :], bias_raw[32:33, :], bias_hi[32:33, :].bitcast(F32),
                                        ALU.subtract).then_inc(bias_ready, 1)

            def split_weights(n, loaded, raw, hi, lo):
                dve.wait_ge(loaded, 16)
                nc.vector.tensor_copy(hi[:], raw).then_inc(prep_chain, 1)
                dve.wait_ge(prep_chain, n + 1)
                nc.vector.tensor_tensor(lo[:], raw, hi[:].bitcast(F32), ALU.subtract
                                        ).then_inc(weights_split, 1)

            def residual(g):
                dve.wait_ge(z_done, g.index + 1)
                dve.wait_ge(xf_in[g.parity], 16 * (g.half + 1))
                x_g = x_feat[:, g.parity]
                nc.vector.scalar_tensor_tensor(x_g, z_ps, gb2_col[:, 0:1], x_g, ALU.add, ALU.add
                                               ).then_inc(x2_ready, 1)
                dve.wait_ge(x2_ready, g.index + 1)
                nc.vector.tensor_copy(x2t[:, bass.ds(g.tokens, GT)], x_g).then_inc(x2_kept, 1)

            def expert_input(g):
                dve.wait_ge(feat_turned, g.index + 1)
                if g.after(2):
                    dve.wait_ge(lg_done, g.index - 1)
                xg_g = xg[:, g.parity]
                nc.vector.tensor_scalar(xg_g, feat_ps, gamma_col[:, 0:1], beta_col[:, 0:1], ALU.mult, ALU.add
                                        ).then_inc(xg_ready, 1)
                dve.wait_ge(xg_ready, g.index + 1)
                hi = xg_hi[:, bass.ds(g.tokens, GT)]
                nc.vector.tensor_copy(hi, xg_g).then_inc(xg_hi_ready, 1)
                dve.wait_ge(xg_hi_ready, g.index + 1)
                nc.vector.tensor_tensor(xg_lo[:, bass.ds(g.tokens, GT)], xg_g, hi.bitcast(F32), ALU.subtract
                                        ).then_inc(xg_lo_ready, 1)

            def stats1(g):
                dve.wait_ge(x_in[g.parity], 16 * (g.half + 1))
                for t in range(TPG):
                    last = nc.vector.bn_stats(bn1[:, t], x_tok[:, g.parity, t])
                last.then_inc(bn1_done, 1)

            def gather1(g):
                for t in range(TPG):
                    last = nc.vector.bn_aggr(mv1[:, g.parity, t], bn1[:, t])
                last.then_inc(stats1_ready, 1)

            def normalise1(g):
                dve.wait_ge(rstd1_ready, g.index + 1)
                if g.after(2):
                    dve.wait_ge(agg_done, g.index - 1)
                for t in range(TPG):
                    last = nc.vector.tensor_scalar(xn1[:, g.parity, t], x_tok[:, g.parity, t],
                                                   mv1[:, g.parity, t, 0:1], rstd1[:, g.parity, t:t + 1],
                                                   ALU.subtract, ALU.mult)
                last.then_inc(xn1_ready, 1)

            def rms_scale(g, t):
                dve.wait_ge(rrms_ready, TPG * g.index + t + 1)
                if g.after(1):
                    dve.wait_ge(hidt_turned, TPG * (g.index - 1) + t + 1)
                nc.vector.scalar_tensor_tensor(hidden[:, t], hid_ps[:, t % 2], rrms[:, g.parity, t:t + 1],
                                               rms_bc, ALU.mult, ALU.mult).then_inc(normed, 1)

            def stats2(g):
                dve.wait_ge(tok_turned, g.index + 1)
                for t in range(TPG):
                    last = nc.vector.bn_stats(bn2[:, t], tok_ps[:, t * P:(t + 1) * P])
                last.then_inc(bn2_done, 1)

            def gather2(g):
                for t in range(TPG):
                    last = nc.vector.bn_aggr(mv2[:, g.parity, t], bn2[:, t])
                last.then_inc(stats2_ready, 1)

            def normalise2(g):
                dve.wait_ge(rstd2_ready, g.index + 1)
                if g.after(1):
                    dve.wait_ge(feat_turned, g.index)
                for t in range(TPG):
                    last = nc.vector.tensor_scalar(xn2[:, t], tok_ps[:, t * P:(t + 1) * P],
                                                   mv2[:, g.parity, t, 0:1], rstd2[:, g.parity, t:t + 1],
                                                   ALU.subtract, ALU.mult)
                last.then_inc(xn2_ready, 1)

            def step(at):
                if g := at(4):
                    residual(g)
                if g := at(5):
                    expert_input(g)
                if g := at(0):
                    stats1(g)
                    dve.wait_ge(bn1_done, g.index + 1)
                if g := at(2):
                    rms_scale(g, 0)
                if g := at(0):
                    gather1(g)
                if g := at(2):
                    rms_scale(g, 1)
                if g := at(0):
                    normalise1(g)
                if g := at(4):
                    stats2(g)
                    dve.wait_ge(bn2_done, g.index + 1)
                if g := at(2):
                    rms_scale(g, 2)
                if g := at(4):
                    gather2(g)
                if g := at(2):
                    rms_scale(g, 3)
                if g := at(4):
                    normalise2(g)
                if g := at(3):
                    if not g.after(1):
                        split_weights(1, w2_in, w2_raw, w2_hi, w2_lo)
                if g := at(2):
                    if not g.after(1):
                        split_weights(0, w1_in, w1_raw, w1_hi, w1_lo)

            prep_bias()
            steps(dve, step)

            links = [0]

            def link(ins):
                links[0] += 1
                ins.then_inc(route_chain, 1)
                dve.wait_ge(route_chain, links[0])

            def spread(col):
                return col.unsqueeze(2).to_broadcast([P, TPQ, E])

            def pick(values, top, chosen):
                link(nc.vector.tensor_reduce(top, values, AX.X, ALU.max))
                link(nc.vector.tensor_tensor(score, values, spread(top), ALU.is_equal))
                link(nc.vector.tensor_tensor(score, score, falling, ALU.mult))
                link(nc.vector.tensor_reduce(place, score, AX.X, ALU.max))
                link(nc.vector.tensor_tensor(chosen, falling, spread(place), ALU.is_equal))

            falling = descend[:].rearrange("p (t e) -> p t e", e=E)
            dve.wait_ge(logits_ready, NG)
            dve.wait_ge(xg_lo_ready, NG)
            for q in range(NQ):
                values = logits[:, q].rearrange("p (t e) -> p t e", e=E)
                pick(values, top1, first)
                link(nc.vector.scalar_tensor_tensor(masked, first, -3.0e38, values, ALU.mult, ALU.add))
                pick(masked, top2, second)
                nc.vector.tensor_tensor(apart, top2, top1, ALU.subtract).then_inc(apart_ready, 1)
                dve.wait_ge(power_ready, q + 1)
                link(nc.vector.tensor_scalar(denom, power, 1.0, None, ALU.add))
                link(nc.vector.reciprocal(share1, denom))
                link(nc.vector.tensor_tensor(share2, share1, power, ALU.mult))
                link(nc.vector.tensor_tensor(first, first, spread(share1), ALU.mult))
                link(nc.vector.tensor_tensor(second, second, spread(share2), ALU.mult))
                nc.vector.tensor_tensor(gates[:, q].rearrange("p (t e) -> p t e", e=E), first, second, ALU.add
                                        ).then_inc(gates_ready, 1)

            def gate(g, u):
                if u == 0:
                    dve.wait_ge(gate_bc_in[g.parity], 16 * (g.half + 1))
                dve.wait_ge(gelu_done, UNITS * g.index + u + 1)
                nc.vector.tensor_tensor(act_out[:, u % 4], act_out[:, u % 4], gate_bc[:, g.parity, u // HCE], ALU.mult
                                        ).then_inc(gated, 1)

            def low_part(g, u):
                dve.wait_ge(hi_ready, UNITS * g.index + u + 1)
                nc.vector.tensor_tensor(h_lo[:, u % 4], act_out[:, u % 4], h_hi[:, u % 4].bitcast(F32), ALU.subtract
                                        ).then_inc(lo_ready, 1)

            def finish(g):
                dve.wait_ge(g_done, UNITS * (g.index + 1))
                x2 = x2t[:, bass.ds(g.tokens, GT)]
                nc.vector.tensor_tensor(x2, y_ps[:, g.parity], x2, ALU.add).then_inc(out_ready, 1)

            def group_units(g, before):
                for u in range(UNITS):
                    gate(g, u)
                    if u >= 1:
                        low_part(g, u - 1)
                    elif before:
                        low_part(before, UNITS - 1)
                    if u == 5 and before:
                        finish(before)

            group_units(Group(0, 0), None)
            group_units(Group(0, 1), Group(0, 0))
            with dve.Fori(0, NG // 2 - 1) as pair:
                for k in range(2):
                    group_units(Group(pair, 2 + k), Group(pair, 1 + k))
            low_part(Group(0, NG - 1), UNITS - 1)
            finish(Group(0, NG - 1))


def kernel(x, adj, L0_gnn_epsilon, L0_gnn_W1, L0_gnn_b1, L0_gnn_rms_weight, L0_gnn_W2, L0_gnn_b2,
           L0_ffn_gamma, L0_ffn_beta, L0_ffn_Wr, L0_ffn_br, L0_ffn_W1, L0_ffn_b1, L0_ffn_W2, L0_ffn_b2):
    import concourse.bacc as bacc
    from concourse.bass_utils import run_bass_kernel_spmd

    x = np.asarray(x)
    arrays = {
        "x": x.reshape(NTOK, D),
        "x_t": x.reshape(NTOK, D).T,
        "adj_t": np.asarray(adj).transpose(0, 2, 1).reshape(NTOK, NODES),
        "eps": np.asarray(L0_gnn_epsilon).reshape(1),
        "gw1": np.asarray(L0_gnn_W1),
        "gb1": np.asarray(L0_gnn_b1).reshape(1, H1),
        "rms_w": np.asarray(L0_gnn_rms_weight),
        "gw2": np.asarray(L0_gnn_W2),
        "gb2": np.asarray(L0_gnn_b2).reshape(D, 1),
        "gamma": np.asarray(L0_ffn_gamma).reshape(D, 1),
        "beta": np.asarray(L0_ffn_beta).reshape(D, 1),
        "wr": np.asarray(L0_ffn_Wr),
        "br": np.asarray(L0_ffn_br).reshape(E, 1),
        "w1": np.asarray(L0_ffn_W1),
        "b1": np.asarray(L0_ffn_b1).reshape(UNITS, P).T,
        "w2": np.asarray(L0_ffn_W2),
        "b2": np.asarray(L0_ffn_b2),
        "ident_in": np.eye(P, dtype=np.float32),
        "descend_in": np.tile(np.arange(E, 0, -1, dtype=np.float32), (P, TPQ)),
    }
    arrays = {k: np.ascontiguousarray(v) for k, v in arrays.items()}
    nc = bacc.Bacc("TRN2", target_bir_lowering=False, num_devices=1)
    args = [nc.dram_tensor(k, v.shape, mybir.dt.from_np(v.dtype), kind="ExternalInput").ap()
            for k, v in arrays.items()]
    out_t = nc.dram_tensor("out_t", (D, NTOK), F32, kind="ExternalOutput").ap()
    build(nc, *args, out_t)
    result = run_bass_kernel_spmd(nc, [arrays], core_ids=[0])
    return np.ascontiguousarray(result.results[0]["out_t"].T).reshape(x.shape)
```

```python
from contextlib import ExitStack

import numpy as np

import concourse.bass as bass
from concourse import mybir

P = 128
D = 128
NTOK = 32 * 256
GT = 512
NG = NTOK // GT
TPG = GT // P
NODES = 256
H1 = 512
HC1 = H1 // P
E = 8
HE = 256
HCE = HE // P
CAP = NTOK + P
ROW = D + 3
AREA = E * CAP + E * P
HALF = NTOK // P + E
TILES = 2 * HALF
LN_EPS = 1e-5
RMS_EPS = 1e-6

F32 = mybir.dt.float32
F32R = mybir.dt.float32r
BF16 = mybir.dt.bfloat16
I32 = mybir.dt.int32
U32 = mybir.dt.uint32
ALU = mybir.AluOpType
ACT = mybir.ActivationFunctionType
AX = mybir.AxisListType

PEEL = 8
MAX_LAG = 8
LOOPS = (NG - PEEL) // 2

RING = 16
SENDS = 8
FIRST_LAG, GELU_LAG, TURN_LAG, LAST_LAG, SEND_LAG = 1, 2, 3, 4, 5
ROUND = 12
PLACE = 4


def constants():
    e = np.arange(E)
    p = np.arange(P)
    parts = {
        "ident": np.eye(P),
        "before": p[:, None] < p[None, :],
        "falling": np.tile(E - e, (P, TPG)),
        "region": np.tile((np.arange(2)[:, None] * AREA + e * CAP).reshape(1, -1), (P, 1)),
        "token": np.arange(TPG)[None, :] * P + p[:, None],
        "unused": NTOK + np.arange(2 * E)[None, :] * P + p[:, None],
        "upto": np.tile((e[None, :] <= e[:, None]).reshape(1, -1), (P, 1)),
        "tile_row": np.tile(np.arange(HALF) * P, (P, 1)),
    }
    parts = {k: np.asarray(v, np.float32).reshape(P, -1) for k, v in parts.items()}
    at, start = {}, 0
    for k, v in parts.items():
        at[k] = (start, v.shape[1])
        start += v.shape[1]
    return np.concatenate(list(parts.values()), 1), at


class Group:

    def __init__(self, pair, offset):
        self.index = pair * 2 + offset
        self.half = pair + offset // 2
        self.parity = offset % 2
        self.tokens = self.index * GT

    def after(self, n):
        return not isinstance(self.index, int) or self.index >= n


def steps(engine, step):
    def peeled(s):
        return lambda lag: Group(0, s - lag) if 0 <= s - lag < NG else None

    for s in range(PEEL):
        step(peeled(s))
    with engine.Fori(0, LOOPS) as pair:
        for k in range(2):
            step(lambda lag, k=k: Group(pair, PEEL + k - lag))
    for s in range(PEEL + 2 * LOOPS, NG + MAX_LAG):
        step(peeled(s))


def build(nc, x, x_t, adj_t, eps, gw1, gb1, rms_w, gw2, gb2, gamma, beta, wr, br, w1, b1, w2, b2,
          fixed_in, out):
    fixed_at = constants()[1]
    with ExitStack() as ctx:
        def sb(name, shape, dt=F32):
            return ctx.enter_context(nc.sbuf_tensor(name, shape, dt))

        def sem(name):
            return ctx.enter_context(nc.semaphore(name))

        w1_sb = sb("w1_sb", [P, E * HE])
        w2_sb = sb("w2_sb", [P, E * HCE * D])
        b1_bc = sb("b1_bc", [P, E * HE])
        b2_bc = sb("b2_bc", [P, E * D])
        fixed = sb("fixed", [P, fixed_in.shape[1]])

        def const(name):
            start, width = fixed_at[name]
            return fixed[:, start:start + width]

        ident, before, region, token, unused, tile_row = map(
            const, ("ident", "before", "region", "token", "unused", "tile_row"))
        falling = const("falling").rearrange("p (t e) -> p t e", e=E)
        upto = const("upto").rearrange("p (e f) -> p e f", f=E)
        eps_col = sb("eps_col", [P, 1])
        gamma_col = sb("gamma_col", [P, 1])
        beta_col = sb("beta_col", [P, 1])
        gb2_col = sb("gb2_col", [P, 1])
        br_col = sb("br_col", [E, 1])
        wr_sb = sb("wr_sb", [P, E])
        minus_half, rms_eps = (sb(name, [P, TPG]) for name in ("minus_half", "rms_eps"))
        euler = sb("euler", [P, TPG])
        bias_sel = sb("bias_sel", [P, P], F32R)
        bias_parts = sb("bias_parts", [P, H1], F32R)
        before_bf = sb("before_bf", [P, P], BF16)
        ones_bf = sb("ones_bf", [P, P], BF16)
        bn1 = sb("bn1", [P, TPG, 6])
        bn2 = sb("bn2", [P, TPG, 6])
        mv1 = sb("mv1", [P, 2, TPG, 2])
        mv2 = sb("mv2", [P, 2, TPG, 2])
        var1 = sb("var1", [P, TPG])
        var2 = sb("var2", [P, TPG])
        rstd1 = sb("rstd1", [P, 2, TPG])
        rstd2 = sb("rstd2", [P, 2, TPG])
        sumsq = sb("sumsq", [P, 2, TPG])
        meansq = sb("meansq", [P, TPG])
        rrms = sb("rrms", [P, 2, TPG])
        logit_rows = sb("logit_rows", [E, GT])
        logits = sb("logits", [P, TPG, E])
        chosen = sb("chosen", [P, TPG + 1, 2, E], BF16)
        masked = sb("masked", [P, TPG, E])
        score = sb("score", [P, TPG, E])
        top1, top2, place, apart, power, denom = (
            sb(name, [P, TPG]) for name in ("top1", "top2", "place", "apart", "power", "denom"))
        share = sb("share", [P, 2, 2, TPG])
        ends = sb("ends", [P, 2, 2 * E])
        rank = sb("rank", [P, TPG, 2 * E])
        ranked = sb("ranked", [P, TPG, 2 * E])
        row_f = sb("row_f", [P, 2 * TPG])
        row_of = sb("row_of", [P, 2, 2 * TPG], U32)
        target = sb("target", [P, TPG])
        ends_i = sb("ends_i", [P, 2 * E], I32)
        fillers = sb("fillers", [P, 2 * E, ROW])
        count_i = sb("count_i", [P, 2 * E], I32)
        padded = sb("padded", [P, 2, E])
        upto_p = sb("upto_p", [P, 2, E, E])
        upto_rows = sb("upto_rows", [P, 2, E])
        jump = sb("jump", [P, 2, E])
        passed = sb("passed", [1, 2, HALF, E])
        jumps = sb("jumps", [1, 2, HALF, E])
        expert_f = sb("expert_f", [1, LAST_LAG + TILES + SEND_LAG])
        first_row_f = sb("first_row_f", [1, 2, HALF])
        first_row = sb("first_row", [1, TILES], I32)
        WORDS = (TILES + SEND_LAG + 1) // 2
        pair_first, pair_last = (sb(name, [1, WORDS]) for name in ("pair_first", "pair_last"))
        word = sb("word", [1, WORDS], I32)

        x_tok = sb("x_tok", [P, 2, TPG, D])
        adj = sb("adj", [P, 2, TPG, NODES])
        x_feat = sb("x_feat", [P, 2, GT])
        xn1 = sb("xn1", [P, 2, TPG, D])
        agg = sb("agg", [P, 2, GT])
        gw1_sb = sb("gw1_sb", [P, H1])
        gw2_sb = sb("gw2_sb", [P, HC1, D])
        rms_bc = sb("rms_bc", [P, H1])
        hidden = sb("hidden", [P, TPG, H1])
        hidden_t = sb("hidden_t", [P, HC1, GT])
        x2 = sb("x2", [P, 2, GT])
        xn2 = sb("xn2", [P, 2, TPG, D])
        xg = sb("xg", [P, 2, GT])
        eps_ident = sb("eps_ident", [P, P])
        rows_out = sb("rows_out", [P, 2, TPG, ROW])
        bias_raw = sb("bias_raw", [P, H1])
        bias_hi = sb("bias_hi", [P, H1], F32R)
        rows_in = sb("rows_in", [P, RING, ROW])
        xg_t = sb("xg_t", [P, 2, P])
        hidden_e = sb("hidden_e", [P, 4, HE])
        hidden_et = sb("hidden_et", [P, 2, HE])
        result = sb("result", [P, SENDS, D])

        rows_dram = nc.dram_tensor("rows_dram", (2 * AREA, ROW), F32).ap()

        banks = ctx.enter_context(nc.psum_tensor("banks", [P, 8, GT], F32))
        agg_ps = z_ps = banks[:, 0]
        hid_ps, hidt_ps = banks[:, 1:5], banks[:, 5]
        tok_ps = feat_ps = banks[:, 6]
        lg_ps = banks[:, 7]
        rank_ps = lg_ps[:, P:P + (TPG + 1) * 2 * E].rearrange("p (t r) -> p t r", r=2 * E)
        xt_ps, h_ps, ht_ps, y_ps = banks[:, 0:2], banks[:, 2:4], banks[:, 4:6], banks[:, 6:8]

        x_in = [sem(f"x_in{p}") for p in range(2)]
        adj_in = [sem(f"adj_in{p}") for p in range(2)]
        xf_in = [sem(f"xf_in{p}") for p in range(2)]
        fixed_in_sbuf = sem("fixed_in_sbuf")
        consts_in = sem("consts_in")
        weights_in = sem("weights_in")
        fills_done = sem("fills_done")
        pool_consts = sem("pool_consts")
        bias_ready = sem("bias_ready")
        rank_consts = sem("rank_consts")
        bn1_done = sem("bn1_done")
        stats1_ready = sem("stats1_ready")
        var1_ready = sem("var1_ready")
        rstd1_ready = sem("rstd1_ready")
        xn1_ready = sem("xn1_ready")
        adj_ready = sem("adj_ready")
        agg_done = sem("agg_done")
        agg_copied = sem("agg_copied")
        hid_done = sem("hid_done")
        sumsq_ready = sem("sumsq_ready")
        meansq_ready = sem("meansq_ready")
        rrms_ready = sem("rrms_ready")
        normed = sem("normed")
        silu_done = sem("silu_done")
        hidt_turned = sem("hidt_turned")
        hidt_copied = sem("hidt_copied")
        z_done = sem("z_done")
        x2_ready = sem("x2_ready")
        tok_turned = sem("tok_turned")
        x2_kept = sem("x2_kept")
        bn2_done = sem("bn2_done")
        stats2_ready = sem("stats2_ready")
        var2_ready = sem("var2_ready")
        rstd2_ready = sem("rstd2_ready")
        xn2_ready = sem("xn2_ready")
        feat_turned = sem("feat_turned")
        xg_ready = sem("xg_ready")
        lg_done = sem("lg_done")
        lg_copied = sem("lg_copied")
        lg_turned = sem("lg_turned")
        logits_ready = sem("logits_ready")
        round_link = sem("round_link")
        apart_ready = sem("apart_ready")
        power_ready = sem("power_ready")
        chosen_ready = sem("chosen_ready")
        ranked_done = sem("ranked_done")
        place_link = sem("place_link")
        targets_used = sem("targets_used")
        place_end = sem("place_end")
        rows_copied = sem("rows_copied")
        x2_stored = [sem(f"x2_stored{p}") for p in range(2)]
        rows_ready = sem("rows_ready")
        rows_sent = [sem(f"rows_sent{p}") for p in range(2)]
        table_link = sem("table_link")
        fillers_ready = sem("fillers_ready")
        fill_sent = [sem(f"fill_sent{c}") for c in range(2)]
        idle_sent = sem("idle_sent")
        unused_cleared = sem("unused_cleared")
        ends_ready = sem("ends_ready")
        table_ready = sem("table_ready")
        rows_here = [sem(f"rows_here{k}") for k in range(RING)]
        xt_turned = sem("xt_turned")
        xg_t_ready = sem("xg_t_ready")
        h_done = sem("h_done")
        h_biased = sem("h_biased")
        gelu_done = sem("gelu_done")
        ht_turned = sem("ht_turned")
        ht_copied = sem("ht_copied")
        y_done = sem("y_done")
        y_biased = sem("y_biased")
        result_ready = sem("result_ready")
        result_sent = [sem(f"result_sent{k}") for k in range(SENDS)]

        x_view = x.rearrange("(g t p) d -> p g t d", p=P, t=TPG)
        adj_view = adj_t.rearrange("(g t p) n -> p g t n", p=P, t=TPG)
        out_view = out[0:NTOK].rearrange("(g t p) d -> p g t d", p=P, t=TPG)
        small_loads = [
            (gw1_sb[:], gw1), (bias_raw[0:1, :], gb1), (bias_raw[32:33, :], gb1),
            (rms_bc[:], rms_w.partition_broadcast(P)),
            (gw2_sb[:], gw2.rearrange("(c p) d -> p c d", p=P)),
            (gb2_col[:], gb2), (gamma_col[:], gamma), (beta_col[:], beta),
            (wr_sb[:], wr), (br_col[:], br),
        ]
        CONSTS = 16 * len(small_loads)
        expert_loads = [
            (w1_sb[:].rearrange("p (e h) -> p e h", e=E), w1.rearrange("e d h -> d e h")),
            (w2_sb[:].rearrange("p (u d) -> p u d", d=D), w2.rearrange("e (c p) d -> p (e c) d", p=P)),
            (b1_bc[:], b1.partition_broadcast(P)), (b2_bc[:], b2.partition_broadcast(P)),
        ]
        WEIGHTS = 16 * len(expert_loads)

        def tile_steps(engine, step):
            def peeled(s):
                return lambda lag: (s - lag, (s - lag) // RING, (s - lag) % RING) if 0 <= s - lag < TILES else None

            middle = HALF // RING * RING
            for start, end in ((0, middle), (middle, TILES)):
                for s in range(start, start + RING):
                    step(peeled(s), s // 2, s % 2)
                first = start // RING + 1
                with engine.Fori(0, end // RING - first) as turn:
                    for k in range(RING):
                        step(lambda lag, k=k: (turn * RING + (first * RING + k - lag),
                                               turn + (first + (k - lag) // RING), (k - lag) % RING),
                             turn * (RING // 2) + (first * RING + k) // 2, k % 2, second=start > 0)
            for s in range(TILES, TILES + SEND_LAG):
                step(peeled(s), s // 2, s % 2)

        def experts_of(w, odd, last_width):
            first_at = (w >> 3 * odd) & (E - 1) * HE
            last_at = (w >> 6 + 3 * odd + HE // last_width - 1) & (E - 1) * last_width
            return (first_at.with_bounds(min_val=0, max_val=(E - 1) * HE),
                    last_at.with_bounds(min_val=0, max_val=(E - 1) * last_width))

        def later(number, n):
            return not isinstance(number, int) or number >= n

        def fill_regions(engine, choice):
            engine.wait_ge(ends_ready, 1)
            for e in range(E):
                r = choice * E + e
                end = engine.value_load(ends_i[0:1, r:r + 1], min_val=0, max_val=2 * AREA - P)
                engine.dma_start(rows_dram[bass.ds(end, P), :], fillers[:, e]).then_inc(fill_sent[choice], 16)

        block = ctx.enter_context(nc.Block())

        @block.sync
        def _(sp):
            def step(at):
                if g := at(0):
                    if g.after(2):
                        sp.wait_ge(xn1_ready, g.index - 1)
                    sp.dma_start(x_tok[:, g.parity], x_view[:, bass.ds(g.index, 1)].squeeze(1)
                                 ).then_inc(x_in[g.parity], 16)
                    if g.after(2):
                        sp.wait_ge(agg_done, g.index - 1)
                    sp.dma_start(adj[:, g.parity], adj_view[:, bass.ds(g.index, 1)].squeeze(1)
                                 ).then_inc(adj_in[g.parity], 16)
                if g := at(2):
                    if g.after(2):
                        sp.wait_ge(tok_turned, g.index - 1)
                    sp.dma_start(x_feat[:, g.parity], x_t[:, bass.ds(g.tokens, GT)]
                                 ).then_inc(xf_in[g.parity], 16)

                if g := at(4):
                    sp.wait_ge(x2_kept, g.index + 1)
                    sp.dma_start(out_view[:, bass.ds(g.index, 1)].squeeze(1),
                                 x2[:, g.parity].rearrange("p (t d) -> p t d", t=TPG)
                                 ).then_inc(x2_stored[g.parity], 16)

            steps(sp, step)
            fill_regions(sp, 0)

            sp.wait_ge(table_ready, 2)
            for p in range(2):
                sp.wait_ge(rows_sent[p], 16 * 2 * TPG * (NG // 2))
            sp.wait_ge(fill_sent[0], 16 * E)
            sp.wait_ge(idle_sent, 16 * 2)

            def load_rows(number, turn, k):
                first = sp.value_load(first_row[0:1, bass.ds(number, 1)], min_val=0, max_val=2 * AREA - P)
                if later(number, RING):
                    sp.wait_ge(result_sent[k % SENDS], 16 * (turn * (RING // SENDS) + k // SENDS - 1))
                sp.dma_start(rows_in[:, k], rows_dram[bass.ds(first, P), :]).then_inc(rows_here[k], 16)

            for k in range(RING):
                load_rows(k, 0, k)
            sp.wait_ge(fill_sent[1], 16 * E)
            with sp.Fori(1, TILES // RING) as turn:
                for k in range(RING):
                    load_rows(turn * RING + k, turn, k)

        @block.gpsimd
        def _(pool):
            nc.gpsimd.memset(minus_half[:], -0.5)
            nc.gpsimd.memset(rms_eps[:], RMS_EPS)
            nc.gpsimd.memset(euler[:], float(np.e)).then_inc(pool_consts, 1)
            pool.wait_ge(pool_consts, 1)

            def send_rows(g, *places):
                for n in places:
                    nc.gpsimd.indirect_dma_start(
                        out=rows_dram,
                        out_offset=bass.IndirectOffsetOnAxis(ap=row_of[:, g.parity, n:n + 1], axis=0),
                        in_=rows_out[:, g.parity, n // 2], in_offset=None).then_inc(rows_sent[g.parity], 16)

            def step(at):
                if g := at(8):
                    send_rows(g, 4, 5, 6, 7)
                if g := at(0):
                    pool.wait_ge(var1_ready, g.index + 1)
                    nc.gpsimd.tensor_tensor(rstd1[:, g.parity], var1[:], minus_half[:], ALU.pow
                                            ).then_inc(rstd1_ready, 1)
                if g := at(7):
                    pool.wait_ge(rows_ready, g.index + 1)
                if g := at(2):
                    pool.wait_ge(sumsq_ready, TPG * (g.index + 1))
                    nc.gpsimd.tensor_tensor(meansq[:], sumsq[:, g.parity], rms_eps[:], ALU.add
                                            ).then_inc(meansq_ready, 1)
                    pool.wait_ge(meansq_ready, g.index + 1)
                    nc.gpsimd.tensor_tensor(rrms[:, g.parity], meansq[:], minus_half[:], ALU.pow
                                            ).then_inc(rrms_ready, 1)
                if g := at(7):
                    send_rows(g, 0, 1)
                if g := at(4):
                    pool.wait_ge(var2_ready, g.index + 1)
                    nc.gpsimd.tensor_tensor(rstd2[:, g.parity], var2[:], minus_half[:], ALU.pow
                                            ).then_inc(rstd2_ready, 1)
                if g := at(7):
                    send_rows(g, 2, 3)
                if g := at(6):
                    pool.wait_ge(apart_ready, g.index + 1)
                    nc.gpsimd.tensor_tensor(power[:], euler[:], apart[:], ALU.pow).then_inc(power_ready, 1)

            pool.wait_ge(fillers_ready, 1)
            for c in range(2):
                pool.dma_start(rows_dram[c * AREA + E * CAP:(c + 1) * AREA].rearrange("(u p) r -> p u r", p=P),
                               fillers[:, E:]).then_inc(idle_sent, 16)
            pool.dma_start(out[NTOK:].rearrange("(u p) d -> p u d", p=P), fillers[:, :, 0:D]
                           ).then_inc(unused_cleared, 16)
            steps(pool, step)
            fill_regions(pool, 1)

            pool.wait_ge(unused_cleared, 16)
            for p in range(2):
                pool.wait_ge(x2_stored[p], 16 * (NG // 2))

            def tile_step(at, pair, odd, second=False):
                sent = at(SEND_LAG)
                if sent and isinstance(sent[0], int) and sent[0] == HALF:
                    for k in range(SENDS):
                        pool.wait_ge(result_sent[k], 16 * (HALF // SENDS))
                if tile := at(LAST_LAG):
                    number, _, k = tile
                    pool.wait_ge(y_biased, number + 1)
                    if later(number, 1):
                        pool.wait_ge(result_ready, number)
                    weight = D + int(number >= HALF if isinstance(number, int) else second)
                    nc.gpsimd.tensor_tensor(result[:, k % SENDS], result[:, k % SENDS],
                                            rows_in[:, k, weight:weight + 1].to_broadcast([P, D]), ALU.mult
                                            ).then_inc(result_ready, 1)
                elif at(SEND_LAG):
                    pool.wait_ge(result_ready, TILES)
                if tile := at(SEND_LAG):
                    number, _, k = tile
                    nc.gpsimd.indirect_dma_start(
                        out=out,
                        out_offset=bass.IndirectOffsetOnAxis(ap=rows_in[:, k, D + 2:D + 3].bitcast(U32), axis=0),
                        in_=result[:, k % SENDS], in_offset=None, compute_op=ALU.add
                    ).then_inc(result_sent[k % SENDS], 16)

            tile_steps(pool, tile_step)
            for k in range(SENDS):
                pool.wait_ge(result_sent[k], 16 * (TILES // SENDS))

        @block.tensor
        def _(pe):
            def aggregate(g):
                pe.wait_ge(xn1_ready, g.index + 1)
                pe.wait_ge(adj_ready, g.index + 1)
                if g.after(1):
                    pe.wait_ge(agg_copied, g.index)
                if g.after(3):
                    pe.wait_ge(x2_ready, g.index - 2)
                for b in range(2):
                    for c in range(2):
                        last = pe.matmul(agg_ps[:, b * NODES:(b + 1) * NODES], xn1[:, g.parity, 2 * b + c],
                                         adj[:, g.parity, 2 * b + c], start=(c == 0), stop=(c == 1))
                last.then_inc(agg_done, 1)

            def widen(g, t):
                if t == 0:
                    pe.wait_ge(agg_copied, g.index + 1)
                    if not g.after(1):
                        pe.wait_ge(bias_ready, 1)
                if g.after(1):
                    pe.wait_ge(normed, TPG * g.index + (t + 1 - TPG))
                pe.matmul(hid_ps[:, t], agg[:, g.parity, t * P:(t + 1) * P], gw1_sb[:], start=True, stop=False)
                pe.matmul(hid_ps[:, t], bias_sel[:], bias_parts[:], start=False, stop=True
                          ).then_inc(hid_done, 1)

            def turn_hidden(g, t):
                pe.wait_ge(silu_done, TPG * g.index + t + 1)
                if t >= 1 or g.after(1):
                    pe.wait_ge(hidt_copied, TPG * g.index + t)
                for c in range(HC1):
                    last = pe.transpose(hidt_ps[:, c * P:(c + 1) * P], hidden[:, t, c * P:(c + 1) * P], ident)
                last.then_inc(hidt_turned, 1)

            def narrow(g):
                pe.wait_ge(hidt_copied, TPG * (g.index + 1))
                pe.wait_ge(agg_copied, min(g.index + 3, NG) if isinstance(g.index, int) else g.index + 3)
                for c in range(HC1):
                    last = pe.matmul(z_ps, gw2_sb[:, c], hidden_t[:, c], start=(c == 0), stop=(c == HC1 - 1))
                last.then_inc(z_done, 1)

            def turn_to_tokens(g):
                pe.wait_ge(x2_ready, g.index + 1)
                if g.after(1):
                    pe.wait_ge(xg_ready, g.index)
                for t in range(TPG):
                    last = pe.transpose(tok_ps[:, t * P:(t + 1) * P], x_feat[:, g.parity, t * P:(t + 1) * P], ident)
                last.then_inc(tok_turned, 1)

            def turn_to_features(g):
                pe.wait_ge(xn2_ready, g.index + 1)
                pe.wait_ge(x2_kept, g.index + 1)
                for t in range(TPG):
                    last = pe.transpose(feat_ps[:, t * P:(t + 1) * P], xn2[:, g.parity, t], ident)
                last.then_inc(feat_turned, 1)

            def router(g):
                pe.wait_ge(xg_ready, g.index + 1)
                if g.after(1):
                    pe.wait_ge(logits_ready, g.index)
                pe.matmul(lg_ps[0:E, :], wr_sb[:], xg[:, g.parity], start=True, stop=True).then_inc(lg_done, 1)

            def turn_logits(g):
                for t in range(TPG):
                    last = pe.transpose(lg_ps[:, t * E:(t + 1) * E], logit_rows[:, t * P:(t + 1) * P],
                                        ident[0:E, 0:E])
                last.then_inc(lg_turned, 1)

            def rank_choices(g):
                pe.wait_ge(chosen_ready, g.index + 1)
                pe.wait_ge(lg_copied, min(g.index + 2, NG) if isinstance(g.index, int) else g.index + 2)
                pe.matmul(rank_ps, before_bf[:], chosen[:].rearrange("p t c e -> p t (c e)"), start=True, stop=True)
                for t in range(TPG):
                    left = TPG - t
                    last = pe.matmul(rank_ps[:, t + 1:], ones_bf[:],
                                     chosen[:, t:t + 1].rearrange("p t c e -> p t (c e)").to_broadcast([P, left, 2 * E]),
                                     start=False, stop=True, skip_group_check=True)
                last.then_inc(ranked_done, 1)

            def step(at):
                for t in range(TPG):
                    if t == 2 and (g := at(6)):
                        pe.wait_ge(lg_copied, g.index + 1)
                        if g.after(1):
                            pe.wait_ge(place_link, PLACE * g.index + (2 - PLACE))
                    if g := at(3):
                        turn_hidden(g, t)
                    if g := at(2):
                        widen(g, t)
                    if t == 0 and (g := at(1)):
                        aggregate(g)
                    if t == 1 and (g := at(7)):
                        rank_choices(g)
                    if t == 1 and (g := at(5)):
                        turn_to_features(g)
                    if t == 2 and (g := at(6)):
                        turn_logits(g)
                    if t == 3 and (g := at(4)):
                        turn_to_tokens(g)
                if g := at(3):
                    narrow(g)
                if g := at(5):
                    router(g)

            pe.wait_ge(fixed_in_sbuf, 32)
            pe.wait_ge(consts_in, CONSTS)
            pe.wait_ge(rank_consts, 1)
            steps(pe, step)

            word_now = [None]

            def tile_step(at, pair, odd, second=False):
                if not odd:
                    word_now[0] = pe.value_load(word[0:1, bass.ds(pair, 1)], min_val=0, max_val=(E ** 4 - 1) * HE)
                first_at, last_at = experts_of(word_now[0], odd, HE)
                if tile := at(0):
                    number, turn, k = tile
                    pe.wait_ge(rows_here[k], 16 * (turn + 1))
                    if later(number, 2):
                        pe.wait_ge(xg_t_ready, number - 1)
                    pe.transpose(xt_ps[:, k % 2, 0:P], rows_in[:, k, 0:D], ident).then_inc(xt_turned, 1)
                if tile := at(FIRST_LAG):
                    number, turn, k = tile
                    pe.wait_ge(xg_t_ready, number + 1)
                    if later(number, 2):
                        pe.wait_ge(h_biased, number - 1)
                    pe.matmul(h_ps[:, k % 2, 0:HE], xg_t[:, k % 2], w1_sb[:, bass.ds(first_at, HE)],
                              start=True, stop=True).then_inc(h_done, 1)
                if tile := at(TURN_LAG):
                    number, turn, k = tile
                    pe.wait_ge(gelu_done, number + 1)
                    if later(number, 2):
                        pe.wait_ge(ht_copied, number - 1)
                    for c in range(HCE):
                        last = pe.transpose(ht_ps[:, k % 2, c * P:(c + 1) * P],
                                            hidden_e[:, k % 4, c * P:(c + 1) * P], ident)
                    last.then_inc(ht_turned, 1)
                if tile := at(LAST_LAG):
                    number, turn, k = tile
                    pe.wait_ge(ht_copied, number + 1)
                    if later(number, 2):
                        pe.wait_ge(y_biased, number - 1)
                    for c in range(HCE):
                        last = pe.matmul(y_ps[:, k % 2, 0:D], hidden_et[:, k % 2, c * P:(c + 1) * P],
                                         w2_sb[:, bass.ds(last_at + c * D, D)],
                                         start=(c == 0), stop=(c == HCE - 1))
                    last.then_inc(y_done, 1)

            pe.wait_ge(weights_in, WEIGHTS)
            pe.wait_ge(table_ready, 2)
            pe.wait_ge(agg_copied, NG)
            pe.wait_ge(normed, TPG * NG)
            pe.wait_ge(hidt_copied, TPG * NG)
            pe.wait_ge(x2_ready, NG)
            pe.wait_ge(xg_ready, NG)
            tile_steps(pe, tile_step)

        @block.scalar
        def _(act):
            act.dma_start(fixed[:], fixed_in).then_inc(fixed_in_sbuf, 16)
            act.dma_start(eps_col[:], eps.partition_broadcast(P)).then_inc(fixed_in_sbuf, 16)
            for dst, src in small_loads:
                act.dma_start(dst, src).then_inc(consts_in, 16)
            for dst, src in expert_loads:
                act.dma_start(dst, src).then_inc(weights_in, 16)

            def silu(g, t):
                act.wait_ge(normed, TPG * g.index + t + 1)
                nc.scalar.activation(hidden[:, t], hidden[:, t], ACT.Silu).then_inc(silu_done, 1)

            def step(at):
                for t in range(TPG):
                    if g := at(3):
                        act.wait_ge(hidt_turned, TPG * g.index + t + 1)
                        if t == 0 and g.after(1):
                            act.wait_ge(z_done, g.index)
                        nc.scalar.activation(hidden_t[:, :, t * P:(t + 1) * P],
                                             hidt_ps.rearrange("p (c k) -> p c k", c=HC1), ACT.Copy
                                             ).then_inc(hidt_copied, 1)
                    if g := at(2):
                        act.wait_ge(hid_done, TPG * g.index + t + 1)
                        nc.scalar.activation(hidden[:, t], hid_ps[:, t], ACT.Square, scale=H1 ** -0.5,
                                             accum_out=sumsq[:, g.parity, t:t + 1]).then_inc(sumsq_ready, 1)
                    if t == 1 and (g := at(1)):
                        act.wait_ge(agg_done, g.index + 1)
                        if g.after(2):
                            act.wait_ge(hid_done, TPG * (g.index - 1))
                        nc.scalar.activation(agg[:, g.parity], agg_ps, ACT.Copy).then_inc(agg_copied, 1)
                    if t == 2 and (g := at(6)):
                        act.wait_ge(lg_turned, g.index + 1)
                        if g.after(1):
                            act.wait_ge(chosen_ready, g.index)
                        nc.scalar.activation(logits[:].rearrange("p t e -> p (t e)"), lg_ps[:, 0:TPG * E], ACT.Copy
                                             ).then_inc(logits_ready, 1)
                    if t == 3 and (g := at(4)):
                        act.wait_ge(tok_turned, g.index + 1)
                        if g.after(2):
                            act.wait_ge(x2_stored[g.parity], 16 * g.half)
                            act.wait_ge(xn2_ready, g.index - 1)
                        nc.scalar.activation(x2[:, g.parity], tok_ps, ACT.Copy).then_inc(x2_kept, 1)
                if g := at(2):
                    for t in range(TPG):
                        silu(g, t)
                if g := at(5):
                    act.wait_ge(lg_done, g.index + 1)
                    nc.scalar.activation(logit_rows[:], lg_ps[0:E, :], ACT.Identity, bias=br_col[:, 0:1]
                                         ).then_inc(lg_copied, 1)
                if g := at(6):
                    if g.after(2):
                        act.wait_ge(rows_sent[g.parity], 16 * 2 * TPG * g.half)
                    nc.scalar.activation(rows_out[:, g.parity, :, 0:D], xn2[:, g.parity], ACT.Copy
                                         ).then_inc(rows_copied, 1)

            act.wait_ge(consts_in, CONSTS)
            steps(act, step)

            def tile_step(at, pair, odd, second=False):
                if tile := at(GELU_LAG):
                    number, turn, k = tile
                    act.wait_ge(h_biased, number + 1)
                    nc.scalar.activation(hidden_e[:, k % 4], hidden_e[:, k % 4], ACT.Gelu).then_inc(gelu_done, 1)
                if tile := at(0):
                    number, turn, k = tile
                    act.wait_ge(xt_turned, number + 1)
                    if later(number, 2):
                        act.wait_ge(h_done, number - 1)
                    nc.scalar.activation(xg_t[:, k % 2], xt_ps[:, k % 2, 0:P], ACT.Identity,
                                         bias=beta_col[:, 0:1], scale=gamma_col[:, 0:1]).then_inc(xg_t_ready, 1)
                if tile := at(TURN_LAG):
                    number, turn, k = tile
                    act.wait_ge(ht_turned, number + 1)
                    if later(number, 2):
                        act.wait_ge(y_done, number - 1)
                    nc.scalar.activation(hidden_et[:, k % 2], ht_ps[:, k % 2, 0:HE], ACT.Copy).then_inc(ht_copied, 1)

            tile_steps(act, tile_step)

        @block.vector
        def _(dve):
            def prep():
                nc.vector.memset(fillers[:, :, 0:D + 2], 0.0)
                nc.vector.memset(expert_f[:], 0.0)
                nc.vector.memset(ones_bf[:], 1.0)
                nc.vector.memset(chosen[:], 0.0)
                nc.vector.memset(bias_sel[:].bitcast(F32), 0.0)
                nc.vector.memset(bias_parts[:].bitcast(F32), 0.0).then_inc(fills_done, 1)
                dve.wait_ge(fills_done, 1)
                for r in (0, 32):
                    nc.vector.memset(bias_sel[r:r + 1, :].bitcast(F32), 1.0)
                dve.wait_ge(fixed_in_sbuf, 32)
                nc.vector.tensor_copy(ends[:, 0], region)
                nc.vector.tensor_copy(target[:], token)
                nc.vector.tensor_copy(fillers[:, :, D + 2].bitcast(U32), unused).then_inc(fillers_ready, 1)
                nc.vector.tensor_copy(before_bf[:], before).then_inc(rank_consts, 1)
                nc.vector.tensor_scalar(eps_ident[:], ident, eps_col[:, 0:1], None, ALU.mult
                                        ).then_inc(fills_done, 1)
                dve.wait_ge(fills_done, 2)

            def prep_bias():
                dve.wait_ge(consts_in, CONSTS)
                nc.vector.tensor_copy(bias_parts[0:1, :], bias_raw[0:1, :])
                nc.vector.tensor_copy(bias_hi[32:33, :], bias_raw[32:33, :]).then_inc(fills_done, 1)
                dve.wait_ge(fills_done, 3)
                nc.vector.tensor_tensor(bias_parts[32:33, :], bias_raw[32:33, :], bias_hi[32:33, :].bitcast(F32),
                                        ALU.subtract).then_inc(bias_ready, 1)

            def residual(g):
                dve.wait_ge(z_done, g.index + 1)
                dve.wait_ge(xf_in[g.parity], 16 * (g.half + 1))
                x_g = x_feat[:, g.parity]
                nc.vector.scalar_tensor_tensor(x_g, z_ps, gb2_col[:, 0:1], x_g, ALU.add, ALU.add
                                               ).then_inc(x2_ready, 1)

            def expert_input(g):
                dve.wait_ge(feat_turned, g.index + 1)
                if g.after(2):
                    dve.wait_ge(lg_done, g.index - 1)
                nc.vector.tensor_scalar(xg[:, g.parity], feat_ps, gamma_col[:, 0:1], beta_col[:, 0:1],
                                        ALU.mult, ALU.add).then_inc(xg_ready, 1)

            def add_epsilon(g):
                dve.wait_ge(adj_in[g.parity], 16 * (g.half + 1))
                for c in range(2):
                    blocks = adj[:, g.parity].rearrange("p (b c) n -> p b c n", c=2)[:, :, c, c * P:(c + 1) * P]
                    last = nc.vector.tensor_tensor(blocks, blocks, eps_ident[:].unsqueeze(1).to_broadcast([P, 2, P]),
                                                   ALU.add)
                last.then_inc(adj_ready, 1)

            def stats1(g):
                dve.wait_ge(x_in[g.parity], 16 * (g.half + 1))
                for t in range(TPG):
                    last = nc.vector.bn_stats(bn1[:, t], x_tok[:, g.parity, t])
                last.then_inc(bn1_done, 1)

            def gather1(g):
                for t in range(TPG):
                    last = nc.vector.bn_aggr(mv1[:, g.parity, t], bn1[:, t])
                last.then_inc(stats1_ready, 1)

            def variance1(g):
                dve.wait_ge(stats1_ready, g.index + 1)
                nc.vector.tensor_scalar(var1[:], mv1[:, g.parity, :, 1], LN_EPS, None, ALU.add
                                        ).then_inc(var1_ready, 1)

            def normalise1(g):
                dve.wait_ge(rstd1_ready, g.index + 1)
                if g.after(2):
                    dve.wait_ge(agg_done, g.index - 1)
                for t in range(TPG):
                    last = nc.vector.tensor_scalar(xn1[:, g.parity, t], x_tok[:, g.parity, t],
                                                   mv1[:, g.parity, t, 0:1], rstd1[:, g.parity, t:t + 1],
                                                   ALU.subtract, ALU.mult)
                last.then_inc(xn1_ready, 1)

            def rms_scale(g, t):
                if t == 0:
                    dve.wait_ge(rrms_ready, g.index + 1)
                nc.vector.scalar_tensor_tensor(hidden[:, t], hid_ps[:, t], rrms[:, g.parity, t:t + 1],
                                               rms_bc[:], ALU.mult, ALU.mult).then_inc(normed, 1)

            def stats2(g):
                dve.wait_ge(x2_kept, g.index + 1)
                for t in range(TPG):
                    last = nc.vector.bn_stats(bn2[:, t], x2[:, g.parity, t * P:(t + 1) * P])
                last.then_inc(bn2_done, 1)

            def gather2(g):
                for t in range(TPG):
                    last = nc.vector.bn_aggr(mv2[:, g.parity, t], bn2[:, t])
                last.then_inc(stats2_ready, 1)

            def variance2(g):
                dve.wait_ge(stats2_ready, g.index + 1)
                nc.vector.tensor_scalar(var2[:], mv2[:, g.parity, :, 1], 1.0 + LN_EPS, LN_EPS * LN_EPS,
                                        ALU.mult, ALU.add).then_inc(var2_ready, 1)

            def normalise2(g):
                dve.wait_ge(rstd2_ready, g.index + 1)
                if g.after(2):
                    dve.wait_ge(rows_copied, g.index - 1)
                for t in range(TPG):
                    last = nc.vector.tensor_scalar(xn2[:, g.parity, t],
                                                   x2[:, g.parity, t * P:(t + 1) * P],
                                                   mv2[:, g.parity, t, 0:1], rstd2[:, g.parity, t:t + 1],
                                                   ALU.subtract, ALU.mult)
                last.then_inc(xn2_ready, 1)

            def spread(col):
                return col[:].unsqueeze(2).to_broadcast([P, TPG, E])

            def largest(g, n, values, top):
                if n:
                    dve.wait_ge(round_link, ROUND * g.index + n)
                nc.vector.tensor_reduce(top[:], values[:], AX.X, ALU.max).then_inc(round_link, 1)

            def where_equal(g, n, values, top, out, link=round_link):
                dve.wait_ge(round_link, ROUND * g.index + n)
                nc.vector.tensor_tensor(out, values, spread(top), ALU.is_equal).then_inc(link, 1)

            def weigh(g, n):
                dve.wait_ge(round_link, ROUND * g.index + n)
                nc.vector.tensor_tensor(score[:], score[:], falling, ALU.mult).then_inc(round_link, 1)

            def take_out_first(g, n):
                dve.wait_ge(round_link, ROUND * g.index + n)
                nc.vector.scalar_tensor_tensor(masked[:], chosen[:, 0:TPG, 0], -3.0e38, logits[:], ALU.mult, ALU.add
                                               ).then_inc(round_link, 1)

            def distance(g):
                dve.wait_ge(round_link, ROUND * g.index + 7)
                nc.vector.tensor_tensor(apart[:], top2[:], top1[:], ALU.subtract).then_inc(apart_ready, 1)

            def shares(g, n):
                if n == 0:
                    dve.wait_ge(power_ready, g.index + 1)
                    nc.vector.tensor_scalar(denom[:], power[:], 1.0, None, ALU.add).then_inc(round_link, 1)
                elif n == 1:
                    dve.wait_ge(round_link, ROUND * g.index + 11)
                    nc.vector.reciprocal(share[:, g.parity, 0], denom[:]).then_inc(round_link, 1)
                else:
                    dve.wait_ge(round_link, ROUND * g.index + 12)
                    nc.vector.tensor_tensor(share[:, g.parity, 1], share[:, g.parity, 0], power[:], ALU.mult)

            def places(g, n):
                p = g.parity
                if n == 0:
                    dve.wait_ge(ranked_done, g.index + 1)
                    nc.vector.tensor_tensor(rank[:], rank_ps[:, 0:TPG],
                                            ends[:, p].unsqueeze(1).to_broadcast([P, TPG, 2 * E]), ALU.add
                                            ).then_inc(place_link, 1)
                    nc.vector.tensor_tensor(ends[:, 1 - p], ends[:, p], rank_ps[:, TPG], ALU.add
                                            ).then_inc(place_link, 1)
                elif n == 1:
                    dve.wait_ge(place_link, PLACE * g.index + 2)
                    nc.vector.tensor_tensor(ranked[:], chosen[:, 0:TPG].rearrange("p t c e -> p t (c e)"), rank[:],
                                            ALU.mult).then_inc(place_link, 1)
                elif n == 2:
                    dve.wait_ge(place_link, PLACE * g.index + 3)
                    nc.vector.tensor_reduce(row_f[:], ranked[:].rearrange("p t (c e) -> p (t c) e", e=E), AX.X,
                                            ALU.add).then_inc(place_link, 1)
                    dve.wait_ge(rows_copied, g.index + 1)
                    nc.vector.tensor_copy(rows_out[:, p, :, D:D + 2], share[:, p].rearrange("p c t -> p t c"))
                    nc.vector.tensor_copy(rows_out[:, p, :, D + 2].bitcast(U32), target[:]
                                          ).then_inc(targets_used, 1)
                else:
                    dve.wait_ge(place_link, PLACE * g.index + 4)
                    nc.vector.tensor_copy(row_of[:, p], row_f[:]).then_inc(rows_ready, 1)
                    dve.wait_ge(targets_used, g.index + 1)
                    nc.vector.tensor_scalar(target[:], target[:], float(GT), None, ALU.add).then_inc(place_end, 1)

            def step(at):
                if g := at(5):
                    normalise2(g)
                if g := at(4):
                    residual(g)
                if g := at(0):
                    stats1(g)
                    dve.wait_ge(bn1_done, g.index + 1)
                if g := at(7):
                    for n in range(3):
                        shares(g, n)
                    places(g, 0)
                if g := at(5):
                    expert_input(g)
                if g := at(0):
                    gather1(g)
                if g := at(7):
                    places(g, 1)
                if g := at(0):
                    variance1(g)
                if g := at(7):
                    places(g, 2)
                if g := at(0):
                    add_epsilon(g)
                if g := at(7):
                    places(g, 3)
                if g := at(6):
                    dve.wait_ge(logits_ready, g.index + 1)
                    largest(g, 0, logits, top1)
                if g := at(0):
                    normalise1(g)
                if g := at(6):
                    where_equal(g, 1, logits[:], top1, score[:])
                if g := at(4):
                    stats2(g)
                    dve.wait_ge(bn2_done, g.index + 1)
                if g := at(6):
                    weigh(g, 2)
                if g := at(2):
                    rms_scale(g, 0)
                if g := at(4):
                    gather2(g)
                if g := at(6):
                    largest(g, 3, score, place)
                if g := at(4):
                    variance2(g)
                if g := at(6):
                    where_equal(g, 4, falling, place, chosen[:, 0:TPG, 0])
                if g := at(2):
                    rms_scale(g, 1)
                if g := at(6):
                    take_out_first(g, 5)
                    largest(g, 6, masked, top2)
                if g := at(2):
                    rms_scale(g, 2)
                if g := at(6):
                    distance(g)
                    where_equal(g, 7, masked[:], top2, score[:])
                if g := at(2):
                    rms_scale(g, 3)
                if g := at(6):
                    weigh(g, 8)
                    largest(g, 9, score, place)
                    where_equal(g, 10, falling, place, chosen[:, 0:TPG, 1], chosen_ready)

            prep()
            prep_bias()
            steps(dve, step)

            links = [0]

            def link(ins):
                links[0] += 1
                ins.then_inc(table_link, 1)
                dve.wait_ge(table_link, links[0])

            dve.wait_ge(place_link, PLACE * NG)
            nc.vector.tensor_copy(ends_i[:], ends[:, 0]).then_inc(ends_ready, 1)
            rows = padded[:].rearrange("p c e -> p (c e)")
            link(nc.vector.tensor_tensor(rows, ends[:, 0], region, ALU.subtract))
            link(nc.vector.tensor_scalar(count_i[:], rows, float(P - 1), None, ALU.add))
            link(nc.vector.tensor_scalar(count_i[:], count_i[:], 7, 7, ALU.logical_shift_right,
                                         ALU.logical_shift_left))
            link(nc.vector.tensor_copy(rows, count_i[:]))
            for c in range(2):
                last = nc.vector.tensor_tensor(upto_p[:, c], upto, padded[:, c:c + 1].to_broadcast([P, E, E]),
                                               ALU.mult)
            link(last)
            link(nc.vector.tensor_reduce(upto_rows[:], upto_p[:], AX.X, ALU.add))
            link(nc.vector.tensor_scalar(jump[:], padded[:], -1.0, float(CAP), ALU.mult, ALU.add))
            tile_of = tile_row[0:1].unsqueeze(2).to_broadcast([1, HALF, E])
            for c in range(2):
                last = nc.vector.tensor_tensor(passed[:, c], tile_of, upto_rows[0:1, c:c + 1].to_broadcast([1, HALF, E]),
                                               ALU.is_ge)
            link(last)
            passed_by = expert_f[:, LAST_LAG:LAST_LAG + TILES].rearrange("p (c i) -> p c i", c=2)
            link(nc.vector.tensor_reduce(passed_by, passed[:], AX.X, ALU.add))
            for c in range(2):
                last = nc.vector.tensor_tensor(jumps[:, c], passed[:, c], jump[0:1, c:c + 1].to_broadcast([1, HALF, E]),
                                               ALU.mult)
            link(last)
            link(nc.vector.tensor_reduce(first_row_f[:], jumps[:], AX.X, ALU.add))
            for c in range(2):
                last = nc.vector.scalar_tensor_tensor(first_row[:, c * HALF:(c + 1) * HALF], first_row_f[:, c],
                                                      float(c * AREA), tile_row[0:1], ALU.add, ALU.add)
            last.then_inc(table_ready, 1)
            link(nc.vector.tensor_scalar(expert_f[:], expert_f[:], float(HE), float((E - 1) * HE), ALU.mult, ALU.min))
            gap = LAST_LAG - FIRST_LAG
            for pairs, start in ((pair_first, gap), (pair_last, 0)):
                by_pair = expert_f[:, start:start + 2 * WORDS].rearrange("p (j o) -> p j o", o=2)
                last = nc.vector.scalar_tensor_tensor(pairs[:], by_pair[:, :, 1], float(E), by_pair[:, :, 0],
                                                      ALU.mult, ALU.add)
            link(last)
            nc.vector.scalar_tensor_tensor(word[:], pair_last[:], float(E * E), pair_first[:], ALU.mult, ALU.add
                                           ).then_inc(table_ready, 1)
            dve.wait_ge(table_ready, 2)

            word_now = [None]

            def tile_step(at, pair, odd, second=False):
                if not odd:
                    word_now[0] = dve.value_load(word[0:1, bass.ds(pair, 1)], min_val=0, max_val=(E ** 4 - 1) * HE)
                first_at, last_at = experts_of(word_now[0], odd, D)
                if tile := at(FIRST_LAG):
                    number, turn, k = tile
                    dve.wait_ge(h_done, number + 1)
                    if later(number, 4):
                        dve.wait_ge(ht_turned, number - 3)
                    nc.vector.tensor_tensor(hidden_e[:, k % 4], h_ps[:, k % 2, 0:HE],
                                            b1_bc[:, bass.ds(first_at, HE)], ALU.add).then_inc(h_biased, 1)
                if tile := at(LAST_LAG):
                    number, turn, k = tile
                    dve.wait_ge(y_done, number + 1)
                    if later(number, SENDS):
                        dve.wait_ge(result_sent[k % SENDS], 16 * (turn * (RING // SENDS) + k // SENDS))
                    nc.vector.tensor_tensor(result[:, k % SENDS], y_ps[:, k % 2, 0:D], b2_bc[:, bass.ds(last_at, D)],
                                            ALU.add).then_inc(y_biased, 1)

            tile_steps(dve, tile_step)


def kernel(x, adj, L0_gnn_epsilon, L0_gnn_W1, L0_gnn_b1, L0_gnn_rms_weight, L0_gnn_W2, L0_gnn_b2,
           L0_ffn_gamma, L0_ffn_beta, L0_ffn_Wr, L0_ffn_br, L0_ffn_W1, L0_ffn_b1, L0_ffn_W2, L0_ffn_b2):
    import concourse.bacc as bacc
    from concourse.bass_utils import run_bass_kernel_spmd

    x = np.asarray(x)
    arrays = {
        "x": x.reshape(NTOK, D),
        "x_t": x.reshape(NTOK, D).T,
        "adj_t": np.asarray(adj).transpose(0, 2, 1).reshape(NTOK, NODES),
        "eps": np.asarray(L0_gnn_epsilon).reshape(1),
        "gw1": np.asarray(L0_gnn_W1),
        "gb1": np.asarray(L0_gnn_b1).reshape(1, H1),
        "rms_w": np.asarray(L0_gnn_rms_weight),
        "gw2": np.asarray(L0_gnn_W2),
        "gb2": np.asarray(L0_gnn_b2).reshape(D, 1),
        "gamma": np.asarray(L0_ffn_gamma).reshape(D, 1),
        "beta": np.asarray(L0_ffn_beta).reshape(D, 1),
        "wr": np.asarray(L0_ffn_Wr),
        "br": np.asarray(L0_ffn_br).reshape(E, 1),
        "w1": np.asarray(L0_ffn_W1),
        "b1": np.asarray(L0_ffn_b1).reshape(E * HE),
        "w2": np.asarray(L0_ffn_W2),
        "b2": np.asarray(L0_ffn_b2).reshape(E * D),
        "fixed_in": constants()[0],
    }
    arrays = {k: np.ascontiguousarray(v) for k, v in arrays.items()}
    nc = bacc.Bacc("TRN2", target_bir_lowering=False, num_devices=1)
    args = [nc.dram_tensor(k, v.shape, mybir.dt.from_np(v.dtype), kind="ExternalInput").ap()
            for k, v in arrays.items()]
    out = nc.dram_tensor("out", (NTOK + 2 * E * P, D), F32, kind="ExternalOutput").ap()
    build(nc, *args, out)
    result = run_bass_kernel_spmd(nc, [arrays], core_ids=[0])
    return np.ascontiguousarray(result.results[0]["out"][:NTOK]).reshape(x.shape)
```

```python
from contextlib import ExitStack

import numpy as np

import concourse.bass as bass
from concourse import mybir

P = 128
D = 128
NTOK = 32 * 256
GT = 512
NG = NTOK // GT
TPG = GT // P
NODES = 256
H1 = 512
HC1 = H1 // P
E = 8
HE = 256
HCE = HE // P
CAP = NTOK + P
ROW = D + 3
AREA = E * CAP + E * P
HALF = NTOK // P + E
TILES = 2 * HALF
LN_EPS = 1e-5
RMS_EPS = 1e-6

F32 = mybir.dt.float32
F32R = mybir.dt.float32r
BF16 = mybir.dt.bfloat16
I32 = mybir.dt.int32
U32 = mybir.dt.uint32
ALU = mybir.AluOpType
ACT = mybir.ActivationFunctionType
AX = mybir.AxisListType

LATE = 4
PEEL = 8
MAX_LAG = 8
LOOPS = (NG - PEEL) // 2

RING = 16
SENDS = 8
FIRST_LAG, GELU_LAG, TURN_LAG, LAST_LAG, SCALE_LAG, SEND_LAG = 1, 2, 3, 4, 5, 6
PER_WORD = 4
ROUND = 12
PLACE = 4


def constants():
    e = np.arange(E)
    p = np.arange(P)
    parts = {
        "ident": np.eye(P),
        "before": p[:, None] < p[None, :],
        "falling": np.tile(E - e, (P, TPG)),
        "region": np.tile((np.arange(2)[:, None] * AREA + e * CAP).reshape(1, -1), (P, 1)),
        "token": np.arange(TPG)[None, :] * P + p[:, None],
        "unused": NTOK + np.arange(2 * E)[None, :] * P + p[:, None],
        "upto": np.tile((e[None, :] <= e[:, None]).reshape(1, -1), (P, 1)),
        "tile_row": p * P,
    }
    parts = {k: np.asarray(v, np.float32).reshape(P, -1) for k, v in parts.items()}
    at, start = {}, 0
    for k, v in parts.items():
        at[k] = (start, v.shape[1])
        start += v.shape[1]
    return np.concatenate(list(parts.values()), 1), at


class Group:

    def __init__(self, pair, offset):
        self.index = pair * 2 + offset
        self.half = pair + offset // 2
        self.parity = offset % 2
        self.tokens = self.index * GT

        self.late = isinstance(self.index, int) and self.index >= NG - LATE
        self.rows = 2 + self.index - (NG - LATE) if self.late else self.parity

    def after(self, n):
        return not isinstance(self.index, int) or self.index >= n


def steps(engine, step):
    def peeled(s):
        return lambda lag: Group(0, s - lag) if 0 <= s - lag < NG else None

    for s in range(PEEL):
        step(peeled(s))
    with engine.Fori(0, LOOPS) as pair:
        for k in range(2):
            step(lambda lag, k=k: Group(pair, PEEL + k - lag))
    for s in range(PEEL + 2 * LOOPS, NG + MAX_LAG):
        step(peeled(s))


def build(nc, x, x_t, adj_t, eps, gw1, gb1, rms_w, gw2, gb2, gamma, beta, wr, br, w1, b1, w2, b2,
          fixed_in, out):
    fixed_at = constants()[1]
    with ExitStack() as ctx:
        def sb(name, shape, dt=F32):
            return ctx.enter_context(nc.sbuf_tensor(name, shape, dt))

        def sem(name):
            return ctx.enter_context(nc.semaphore(name))

        w1_sb = sb("w1_sb", [P, E * HE])
        w2_sb = sb("w2_sb", [P, E * HCE * D])
        b1_bc = sb("b1_bc", [P, E * HE])
        b2_bc = sb("b2_bc", [P, E * D])
        fixed = sb("fixed", [P, fixed_in.shape[1]])

        def const(name):
            start, width = fixed_at[name]
            return fixed[:, start:start + width]

        ident, before, region, token, unused, tile_row = map(
            const, ("ident", "before", "region", "token", "unused", "tile_row"))
        falling = const("falling").rearrange("p (t e) -> p t e", e=E)
        upto = const("upto").rearrange("p (e f) -> p e f", f=E)
        eps_col = sb("eps_col", [P, 1])
        gamma_col = sb("gamma_col", [P, 1])
        beta_col = sb("beta_col", [P, 1])
        gb2_col = sb("gb2_col", [P, 1])
        br_col = sb("br_col", [E, 1])
        wr_sb = sb("wr_sb", [P, E])
        minus_half, rms_eps = (sb(name, [P, TPG]) for name in ("minus_half", "rms_eps"))
        euler = sb("euler", [P, TPG])
        bias_sel = sb("bias_sel", [P, P], F32R)
        bias_parts = sb("bias_parts", [P, H1], F32R)
        before_bf = sb("before_bf", [P, P], BF16)
        ones_bf = sb("ones_bf", [P, P], BF16)
        bn1 = sb("bn1", [P, TPG, 6])
        bn2 = sb("bn2", [P, TPG, 6])
        mv1 = sb("mv1", [P, 2, TPG, 2])
        mv2 = sb("mv2", [P, 2, TPG, 2])
        var1 = sb("var1", [P, TPG])
        var2 = sb("var2", [P, TPG])
        rstd1 = sb("rstd1", [P, 2, TPG])
        rstd2 = sb("rstd2", [P, 2, TPG])
        sumsq = sb("sumsq", [P, 2, TPG])
        meansq = sb("meansq", [P, TPG])
        rrms = sb("rrms", [P, 2, TPG])
        logit_rows = sb("logit_rows", [E, GT])
        logits = sb("logits", [P, TPG, E])
        chosen = sb("chosen", [P, TPG + 1, 2, E], BF16)
        masked = sb("masked", [P, TPG, E])
        score = sb("score", [P, TPG, E])
        top1, top2, place, apart, power, denom = (
            sb(name, [P, TPG]) for name in ("top1", "top2", "place", "apart", "power", "denom"))
        share = sb("share", [P, 2, 2, TPG])
        ends = sb("ends", [P, 2, 2 * E])
        rank = sb("rank", [P, TPG, 2 * E])
        ranked = sb("ranked", [P, TPG, 2 * E])
        row_f = sb("row_f", [P, 2 * TPG])
        row_of = sb("row_of", [P, 2 + LATE, 2 * TPG], U32)
        target = sb("target", [P, TPG])
        ends_i = sb("ends_i", [P, 2 * E], I32)
        fillers = sb("fillers", [P, 2 * E, ROW])
        count_i = sb("count_i", [P, 2 * E], I32)
        padded = sb("padded", [P, 2, E])
        upto_p = sb("upto_p", [P, 2, E, E])
        upto_rows = sb("upto_rows", [P, 2, E])
        jump = sb("jump", [P, 2, E])
        passed = sb("passed", [P, 2, E])
        jumps = sb("jumps", [P, 2, E])
        columns = sb("columns", [P, 4])
        WORDS = -(-(TILES + SEND_LAG) // PER_WORD)
        FIELDS = LAST_LAG - FIRST_LAG + PER_WORD
        expert_f = sb("expert_f", [1, LAST_LAG + TILES + 2 * PER_WORD])
        first_row = sb("first_row", [1, TILES], I32)
        two_f, four_f = sb("two_f", [1, 3, WORDS]), sb("four_f", [1, 2, WORDS])
        word = sb("word", [1, WORDS], I32)

        x_tok = sb("x_tok", [P, 2, TPG, D])
        adj = sb("adj", [P, 2, TPG, NODES])
        x_feat = sb("x_feat", [P, 2, GT])
        xn1 = sb("xn1", [P, 2, TPG, D])
        agg = sb("agg", [P, 2, GT])
        gw1_sb = sb("gw1_sb", [P, H1])
        gw2_sb = sb("gw2_sb", [P, HC1, D])
        rms_bc = sb("rms_bc", [P, H1])
        hidden = sb("hidden", [P, TPG, H1])
        hidden_t = sb("hidden_t", [P, HC1, GT])
        x2 = sb("x2", [P, 2, GT])
        xn2 = sb("xn2", [P, 2, TPG, D])
        xg = sb("xg", [P, 2, GT])
        eps_ident = sb("eps_ident", [P, P])
        rows_out = sb("rows_out", [P, 2 + LATE, TPG, ROW])
        bias_raw = sb("bias_raw", [P, H1])
        bias_hi = sb("bias_hi", [P, H1], F32R)
        rows_in = sb("rows_in", [P, RING, ROW])
        xg_t = sb("xg_t", [P, 2, P])
        hidden_e = sb("hidden_e", [P, 4, HE])
        hidden_et = sb("hidden_et", [P, 2, HE])
        result = sb("result", [P, SENDS, D])
        zero_col = sb("zero_col", [P, 1], U32)
        numbers = sb("numbers", [P, RING, 1], U32)

        rows_dram = nc.dram_tensor("rows_dram", (2 * AREA, ROW), F32).ap()

        banks = ctx.enter_context(nc.psum_tensor("banks", [P, 8, GT], F32))
        agg_ps = z_ps = banks[:, 0]
        hid_ps, hidt_ps = banks[:, 1:5], banks[:, 5]
        tok_ps = feat_ps = banks[:, 6]
        lg_ps = banks[:, 7]
        rank_ps = lg_ps[:, P:P + (TPG + 1) * 2 * E].rearrange("p (t r) -> p t r", r=2 * E)
        column_ps = banks[0:1, 1].rearrange("p (u i) -> p u i", u=4)
        xt_ps, h_ps, ht_ps, y_ps = banks[:, 0:2], banks[:, 2:4], banks[:, 4:6], banks[:, 6:8]

        x_in = [sem(f"x_in{p}") for p in range(2)]
        adj_in = [sem(f"adj_in{p}") for p in range(2)]
        xf_in = [sem(f"xf_in{p}") for p in range(2)]
        fixed_in_sbuf = sem("fixed_in_sbuf")
        consts_in = sem("consts_in")
        weights_in = sem("weights_in")
        fills_done = sem("fills_done")
        pool_consts = sem("pool_consts")
        bias_ready = sem("bias_ready")
        rank_consts = sem("rank_consts")
        bn1_done = sem("bn1_done")
        stats1_ready = sem("stats1_ready")
        var1_ready = sem("var1_ready")
        rstd1_ready = sem("rstd1_ready")
        xn1_ready = sem("xn1_ready")
        adj_ready = sem("adj_ready")
        agg_done = sem("agg_done")
        agg_copied = sem("agg_copied")
        hid_done = sem("hid_done")
        sumsq_ready = sem("sumsq_ready")
        meansq_ready = sem("meansq_ready")
        rrms_ready = sem("rrms_ready")
        normed = sem("normed")
        silu_done = sem("silu_done")
        hidt_turned = sem("hidt_turned")
        hidt_copied = sem("hidt_copied")
        z_done = sem("z_done")
        x2_ready = sem("x2_ready")
        tok_turned = sem("tok_turned")
        x2_kept = sem("x2_kept")
        bn2_done = sem("bn2_done")
        stats2_ready = sem("stats2_ready")
        var2_ready = sem("var2_ready")
        rstd2_ready = sem("rstd2_ready")
        xn2_ready = sem("xn2_ready")
        feat_turned = sem("feat_turned")
        xg_ready = sem("xg_ready")
        lg_done = sem("lg_done")
        lg_copied = sem("lg_copied")
        lg_turned = sem("lg_turned")
        logits_ready = sem("logits_ready")
        round_link = sem("round_link")
        apart_ready = sem("apart_ready")
        power_ready = sem("power_ready")
        chosen_ready = sem("chosen_ready")
        shares_ready = sem("shares_ready")
        ranked_done = sem("ranked_done")
        place_link = sem("place_link")
        targets_used = sem("targets_used")
        place_end = sem("place_end")
        rows_copied = sem("rows_copied")
        x2_stored = [sem(f"x2_stored{p}") for p in range(2)]
        rows_ready = sem("rows_ready")
        rows_sent = [sem(f"rows_sent{p}") for p in range(2)]
        late_sent = [sem(f"late_sent{c}") for c in range(2)]
        table_link = sem("table_link")
        fillers_ready = sem("fillers_ready")
        fill_sent = [sem(f"fill_sent{c}") for c in range(2)]
        idle_sent = sem("idle_sent")
        unused_cleared = sem("unused_cleared")
        ends_ready = sem("ends_ready")
        columns_ready = sem("columns_ready")
        columns_turned = sem("columns_turned")
        table_ready = sem("table_ready")
        rows_here = [sem(f"rows_here{k}") for k in range(RING)]
        xt_turned = sem("xt_turned")
        xg_t_ready = sem("xg_t_ready")
        h_done = sem("h_done")
        h_biased = sem("h_biased")
        gelu_done = sem("gelu_done")
        ht_turned = sem("ht_turned")
        ht_copied = sem("ht_copied")
        y_done = sem("y_done")
        y_biased = sem("y_biased")
        result_ready = sem("result_ready")
        numbers_ready = sem("numbers_ready")
        result_sent = [sem(f"result_sent{k}") for k in range(SENDS)]

        x_view = x.rearrange("(g t p) d -> p g t d", p=P, t=TPG)
        adj_view = adj_t.rearrange("(g t p) n -> p g t n", p=P, t=TPG)
        out_view = out[0:NTOK].rearrange("(g t p) d -> p g t d", p=P, t=TPG)
        small_loads = [
            (gw1_sb[:], gw1), (bias_raw[0:1, :], gb1), (bias_raw[32:33, :], gb1),
            (rms_bc[:], rms_w.partition_broadcast(P)),
            (gw2_sb[:], gw2.rearrange("(c p) d -> p c d", p=P)),
            (gb2_col[:], gb2), (gamma_col[:], gamma), (beta_col[:], beta),
            (wr_sb[:], wr), (br_col[:], br),
        ]
        CONSTS = 16 * len(small_loads)
        expert_loads = [
            (w1_sb[:].rearrange("p (e h) -> p e h", e=E), w1.rearrange("e d h -> d e h")),
            (w2_sb[:].rearrange("p (u d) -> p u d", d=D), w2.rearrange("e (c p) d -> p (e c) d", p=P)),
            (b1_bc[:], b1.partition_broadcast(P)), (b2_bc[:], b2.partition_broadcast(P)),
        ]
        WEIGHTS = 16 * len(expert_loads)

        def tile_steps(engine, step):
            def peeled(s):
                return lambda lag: (s - lag, (s - lag) // RING, (s - lag) % RING) if 0 <= s - lag < TILES else None

            middle = HALF // RING * RING
            for start, end in ((0, middle), (middle, TILES)):
                for s in range(start, start + RING):
                    step(peeled(s), s // PER_WORD, s % PER_WORD)
                first = start // RING + 1
                with engine.Fori(0, end // RING - first) as turn:
                    for k in range(RING):
                        step(lambda lag, k=k: (turn * RING + (first * RING + k - lag),
                                               turn + (first + (k - lag) // RING), (k - lag) % RING),
                             turn * (RING // PER_WORD) + (first * RING + k) // PER_WORD, k % PER_WORD, second=start > 0)
            for s in range(TILES, TILES + SEND_LAG):
                step(peeled(s), s // PER_WORD, s % PER_WORD)

        def experts_of(w, q, last_width):
            def start(field, width):
                shift = width.bit_length() - 1 - 3 * field
                moved = w << shift if shift >= 0 else w >> -shift
                return (moved & (E - 1) * width).with_bounds(min_val=0, max_val=(E - 1) * width)

            return start(q + LAST_LAG - FIRST_LAG, HE), start(q, last_width)

        def later(number, n):
            return not isinstance(number, int) or number >= n

        def fill_regions(engine, choice):
            engine.wait_ge(ends_ready, 1)
            for e in range(E):
                r = choice * E + e
                end = engine.value_load(ends_i[0:1, r:r + 1], min_val=0, max_val=2 * AREA - P)
                engine.dma_start(rows_dram[bass.ds(end, P), :], fillers[:, e]).then_inc(fill_sent[choice], 16)

        block = ctx.enter_context(nc.Block())

        @block.sync
        def _(sp):
            def step(at):
                if g := at(0):
                    if g.after(2):
                        sp.wait_ge(xn1_ready, g.index - 1)
                    sp.dma_start(x_tok[:, g.parity], x_view[:, bass.ds(g.index, 1)].squeeze(1)
                                 ).then_inc(x_in[g.parity], 16)
                    if g.after(2):
                        sp.wait_ge(agg_done, g.index - 1)
                    sp.dma_start(adj[:, g.parity], adj_view[:, bass.ds(g.index, 1)].squeeze(1)
                                 ).then_inc(adj_in[g.parity], 16)
                if g := at(2):
                    if g.after(2):
                        sp.wait_ge(tok_turned, g.index - 1)
                    sp.dma_start(x_feat[:, g.parity], x_t[:, bass.ds(g.tokens, GT)]
                                 ).then_inc(xf_in[g.parity], 16)

                if g := at(4):
                    sp.wait_ge(x2_kept, g.index + 1)
                    sp.dma_start(out_view[:, bass.ds(g.index, 1)].squeeze(1),
                                 x2[:, g.parity].rearrange("p (t d) -> p t d", t=TPG)
                                 ).then_inc(x2_stored[g.parity], 16)

            steps(sp, step)
            fill_regions(sp, 0)

            sp.wait_ge(table_ready, 2)
            for p in range(2):
                sp.wait_ge(rows_sent[p], 16 * 2 * TPG * len(range(p, NG - LATE, 2)))
            sp.wait_ge(late_sent[0], 16 * TPG * LATE)
            sp.wait_ge(fill_sent[0], 16 * E)
            sp.wait_ge(idle_sent, 16 * 2)

            def load_rows(number, turn, k):
                first = sp.value_load(first_row[0:1, bass.ds(number, 1)], min_val=0, max_val=2 * AREA - P)
                if later(number, RING):
                    sp.wait_ge(result_sent[k % SENDS], 16 * (turn * (RING // SENDS) + k // SENDS - 1))
                sp.dma_start(rows_in[:, k], rows_dram[bass.ds(first, P), :]).then_inc(rows_here[k], 16)

            for k in range(RING):
                load_rows(k, 0, k)
            fill_regions(sp, 1)
            with sp.Fori(1, HALF // RING) as turn:
                for k in range(RING):
                    load_rows(turn * RING + k, turn, k)
            sp.wait_ge(late_sent[1], 16 * TPG * LATE)
            sp.wait_ge(fill_sent[1], 16 * E)
            with sp.Fori(HALF // RING, TILES // RING) as turn:
                for k in range(RING):
                    load_rows(turn * RING + k, turn, k)

        @block.gpsimd
        def _(pool):
            nc.gpsimd.memset(minus_half[:], -0.5)
            nc.gpsimd.memset(zero_col[:], 0)
            nc.gpsimd.memset(rms_eps[:], RMS_EPS)
            nc.gpsimd.memset(euler[:], float(np.e)).then_inc(pool_consts, 1)
            pool.wait_ge(pool_consts, 1)

            def send_rows(g, *places):
                for n in places:
                    nc.gpsimd.indirect_dma_start(
                        out=rows_dram,
                        out_offset=bass.IndirectOffsetOnAxis(ap=row_of[:, g.rows, n:n + 1], axis=0),
                        in_=rows_out[:, g.rows, n // 2], in_offset=None
                    ).then_inc(late_sent[n % 2] if g.late else rows_sent[g.parity], 16)

            def step(at):
                if (g := at(3)) and not g.after(1):
                    pool.wait_ge(fillers_ready, 1)
                    for c in range(2):
                        pool.dma_start(rows_dram[c * AREA + E * CAP:(c + 1) * AREA].rearrange("(u p) r -> p u r", p=P),
                                       fillers[:, E:]).then_inc(idle_sent, 16)
                    pool.dma_start(out[NTOK:].rearrange("(u p) d -> p u d", p=P), fillers[:, :, 0:D]
                                   ).then_inc(unused_cleared, 16)
                if (g := at(8)) and not g.late:
                    send_rows(g, 6, 7)
                if g := at(7):
                    pool.wait_ge(rows_ready, g.index + 1)
                if g := at(0):
                    pool.wait_ge(var1_ready, g.index + 1)
                    nc.gpsimd.tensor_tensor(rstd1[:, g.parity], var1[:], minus_half[:], ALU.pow
                                            ).then_inc(rstd1_ready, 1)
                if (g := at(7)) and not g.late:
                    send_rows(g, 0, 1)
                if g := at(6):
                    pool.wait_ge(apart_ready, g.index + 1)
                    nc.gpsimd.tensor_tensor(power[:], euler[:], apart[:], ALU.pow).then_inc(power_ready, 1)
                if g := at(2):
                    pool.wait_ge(sumsq_ready, TPG * (g.index + 1))
                    nc.gpsimd.tensor_tensor(meansq[:], sumsq[:, g.parity], rms_eps[:], ALU.add
                                            ).then_inc(meansq_ready, 1)
                    pool.wait_ge(meansq_ready, g.index + 1)
                    nc.gpsimd.tensor_tensor(rrms[:, g.parity], meansq[:], minus_half[:], ALU.pow
                                            ).then_inc(rrms_ready, 1)
                if (g := at(7)) and not g.late:
                    send_rows(g, 2, 3)
                if g := at(4):
                    pool.wait_ge(var2_ready, g.index + 1)
                    nc.gpsimd.tensor_tensor(rstd2[:, g.parity], var2[:], minus_half[:], ALU.pow
                                            ).then_inc(rstd2_ready, 1)
                if (g := at(7)) and not g.late:
                    send_rows(g, 4, 5)
                if (g := at(7)) and g.late:
                    send_rows(g, 0, 2, 4, 6)

            steps(pool, step)
            for index in range(NG - LATE, NG):
                send_rows(Group(0, index), 1, 3, 5, 7)

            pool.wait_ge(unused_cleared, 16)
            for p in range(2):
                pool.wait_ge(x2_stored[p], 16 * (NG // 2))

            def tile_step(at, quad, q, second=False):
                sent = at(SEND_LAG)
                if sent and isinstance(sent[0], int) and sent[0] == HALF:
                    for k in range(SENDS):
                        pool.wait_ge(result_sent[k], 16 * (HALF // SENDS))
                if tile := at(SCALE_LAG):
                    number, _, k = tile
                    if later(number, 1):
                        pool.wait_ge(numbers_ready, number)
                        pool.wait_ge(result_ready, number)
                    pool.wait_ge(xt_turned, number + 1)
                    nc.gpsimd.tensor_tensor(numbers[:, k], rows_in[:, k, D + 2:D + 3].bitcast(U32), zero_col[:], ALU.add
                                            ).then_inc(numbers_ready, 1)
                elif at(SEND_LAG):
                    pool.wait_ge(numbers_ready, TILES)
                    pool.wait_ge(result_ready, TILES)
                if tile := at(SEND_LAG):
                    number, _, k = tile
                    nc.gpsimd.indirect_dma_start(
                        out=out,
                        out_offset=bass.IndirectOffsetOnAxis(ap=numbers[:, k], axis=0),
                        in_=result[:, k % SENDS], in_offset=None, compute_op=ALU.add
                    ).then_inc(result_sent[k % SENDS], 16)

            tile_steps(pool, tile_step)
            for k in range(SENDS):
                pool.wait_ge(result_sent[k], 16 * (TILES // SENDS))

        @block.tensor
        def _(pe):
            def aggregate(g):
                pe.wait_ge(xn1_ready, g.index + 1)
                pe.wait_ge(adj_ready, g.index + 1)
                if g.after(1):
                    pe.wait_ge(agg_copied, g.index)
                if g.after(3):
                    pe.wait_ge(x2_ready, g.index - 2)
                for b in range(2):
                    for c in range(2):
                        last = pe.matmul(agg_ps[:, b * NODES:(b + 1) * NODES], xn1[:, g.parity, 2 * b + c],
                                         adj[:, g.parity, 2 * b + c], start=(c == 0), stop=(c == 1))
                last.then_inc(agg_done, 1)

            def widen(g, t):
                if t == 0:
                    pe.wait_ge(agg_copied, g.index + 1)
                    if not g.after(1):
                        pe.wait_ge(consts_in, CONSTS)
                        pe.wait_ge(bias_ready, 1)
                        pe.wait_ge(rank_consts, 1)
                if g.after(1):
                    pe.wait_ge(normed, TPG * g.index + (t + 1 - TPG))
                pe.matmul(hid_ps[:, t], agg[:, g.parity, t * P:(t + 1) * P], gw1_sb[:], start=True, stop=False)
                pe.matmul(hid_ps[:, t], bias_sel[:], bias_parts[:], start=False, stop=True
                          ).then_inc(hid_done, 1)

            def turn_hidden(g, t):
                pe.wait_ge(silu_done, TPG * g.index + t + 1)
                if t >= 1 or g.after(1):
                    pe.wait_ge(hidt_copied, TPG * g.index + t)
                for c in range(HC1):
                    last = pe.transpose(hidt_ps[:, c * P:(c + 1) * P], hidden[:, t, c * P:(c + 1) * P], ident)
                last.then_inc(hidt_turned, 1)

            def narrow(g, chunks):
                for c in chunks:
                    if c == 0:
                        pe.wait_ge(hidt_copied, TPG * (g.index + 1))
                        pe.wait_ge(agg_copied, min(g.index + 3, NG) if isinstance(g.index, int) else g.index + 3)
                    last = pe.matmul(z_ps, gw2_sb[:, c], hidden_t[:, c], start=(c == 0), stop=(c == HC1 - 1))
                if c == HC1 - 1:
                    last.then_inc(z_done, 1)

            def turn_to_tokens(g):
                pe.wait_ge(x2_ready, g.index + 1)
                if g.after(1):
                    pe.wait_ge(xg_ready, g.index)
                for t in range(TPG):
                    last = pe.transpose(tok_ps[:, t * P:(t + 1) * P], x_feat[:, g.parity, t * P:(t + 1) * P], ident)
                last.then_inc(tok_turned, 1)

            def turn_to_features(g):
                pe.wait_ge(xn2_ready, g.index + 1)
                pe.wait_ge(x2_kept, g.index + 1)
                for t in range(TPG):
                    last = pe.transpose(feat_ps[:, t * P:(t + 1) * P], xn2[:, g.parity, t], ident)
                last.then_inc(feat_turned, 1)

            def router(g):
                pe.wait_ge(xg_ready, g.index + 1)
                if g.after(1):
                    pe.wait_ge(logits_ready, g.index)
                pe.matmul(lg_ps[0:E, :], wr_sb[:], xg[:, g.parity], start=True, stop=True).then_inc(lg_done, 1)

            def turn_logits(g):
                for t in range(TPG):
                    last = pe.transpose(lg_ps[:, t * E:(t + 1) * E], logit_rows[:, t * P:(t + 1) * P],
                                        ident[0:E, 0:E])
                last.then_inc(lg_turned, 1)

            def rank_choices(g):
                pe.wait_ge(chosen_ready, g.index + 1)
                pe.wait_ge(lg_copied, min(g.index + 2, NG) if isinstance(g.index, int) else g.index + 2)
                pe.matmul(rank_ps, before_bf[:], chosen[:].rearrange("p t c e -> p t (c e)"), start=True, stop=True)
                for t in range(TPG):
                    left = TPG - t
                    last = pe.matmul(rank_ps[:, t + 1:], ones_bf[:],
                                     chosen[:, t:t + 1].rearrange("p t c e -> p t (c e)").to_broadcast([P, left, 2 * E]),
                                     start=False, stop=True, skip_group_check=True)
                last.then_inc(ranked_done, 1)

            def step(at):
                for t in range(TPG):
                    if g := at(3):
                        turn_hidden(g, t)
                    if g := at(2):
                        widen(g, t)
                    if t == 1 and (g := at(5)):
                        turn_to_features(g)
                    if t == 1 and (g := at(1)):
                        aggregate(g)
                    if t == 2 and (g := at(5)):
                        router(g)
                    if t == 3 and (g := at(4)):
                        turn_to_tokens(g)
                    if t == 3 and (g := at(6)):
                        rank_choices(g)
                if g := at(3):
                    narrow(g, range(HC1 - 1))
                if g := at(5):
                    pe.wait_ge(lg_copied, g.index + 1)
                    if g.after(1):
                        pe.wait_ge(place_link, PLACE * g.index + (2 - PLACE))
                if g := at(3):
                    narrow(g, [HC1 - 1])
                if g := at(5):
                    turn_logits(g)

            pe.wait_ge(fixed_in_sbuf, 32)
            steps(pe, step)
            pe.wait_ge(columns_ready, 1)
            pe.wait_ge(normed, TPG * NG)
            for u in range(4):
                last = pe.transpose(column_ps[:, u], columns[:, u:u + 1], ident)
            last.then_inc(columns_turned, 1)

            word_now = [None]

            def tile_step(at, quad, q, second=False):
                if q == 0:
                    word_now[0] = pe.value_load(word[0:1, bass.ds(quad, 1)], min_val=0, max_val=E ** FIELDS - 1)
                first_at, last_at = experts_of(word_now[0], q, HE)
                if tile := at(0):
                    number, turn, k = tile
                    pe.wait_ge(rows_here[k], 16 * (turn + 1))
                    pe.transpose(xt_ps[:, k % 2, 0:P], rows_in[:, k, 0:D], ident).then_inc(xt_turned, 1)
                if tile := at(TURN_LAG):
                    number, turn, k = tile
                    pe.wait_ge(gelu_done, number + 1)
                    for c in range(HCE):
                        last = pe.transpose(ht_ps[:, k % 2, c * P:(c + 1) * P],
                                            hidden_e[:, k % 4, c * P:(c + 1) * P], ident)
                    last.then_inc(ht_turned, 1)
                if tile := at(FIRST_LAG):
                    number, turn, k = tile
                    pe.wait_ge(xg_t_ready, number + 1)
                    pe.matmul(h_ps[:, k % 2, 0:HE], xg_t[:, k % 2], w1_sb[:, bass.ds(first_at, HE)],
                              start=True, stop=True).then_inc(h_done, 1)
                if tile := at(LAST_LAG):
                    number, turn, k = tile
                    pe.wait_ge(ht_copied, number + 1)
                    if later(number, 2):
                        pe.wait_ge(y_biased, number - 1)
                    for c in range(HCE):
                        last = pe.matmul(y_ps[:, k % 2, 0:D], hidden_et[:, k % 2, c * P:(c + 1) * P],
                                         w2_sb[:, bass.ds(last_at + c * D, D)],
                                         start=(c == 0), stop=(c == HCE - 1))
                    last.then_inc(y_done, 1)

            pe.wait_ge(weights_in, WEIGHTS)
            pe.wait_ge(table_ready, 2)
            pe.wait_ge(agg_copied, NG)
            pe.wait_ge(normed, TPG * NG)
            pe.wait_ge(hidt_copied, TPG * NG)
            pe.wait_ge(x2_ready, NG)
            pe.wait_ge(xg_ready, NG)
            tile_steps(pe, tile_step)

        @block.scalar
        def _(act):
            act.dma_start(fixed[:], fixed_in).then_inc(fixed_in_sbuf, 16)
            act.dma_start(eps_col[:], eps.partition_broadcast(P)).then_inc(fixed_in_sbuf, 16)
            for dst, src in small_loads:
                act.dma_start(dst, src).then_inc(consts_in, 16)

            def silu(g, t):
                act.wait_ge(normed, TPG * g.index + t + 1)
                nc.scalar.activation(hidden[:, t], hidden[:, t], ACT.Silu).then_inc(silu_done, 1)

            def step(at):
                if (g := at(4)) and not g.after(1):
                    for dst, src in expert_loads:
                        act.dma_start(dst, src).then_inc(weights_in, 16)
                for t in range(TPG):
                    if g := at(3):
                        act.wait_ge(hidt_turned, TPG * g.index + t + 1)
                        if t == 0 and g.after(1):
                            act.wait_ge(z_done, g.index)
                        nc.scalar.activation(hidden_t[:, :, t * P:(t + 1) * P],
                                             hidt_ps.rearrange("p (c k) -> p c k", c=HC1), ACT.Copy
                                             ).then_inc(hidt_copied, 1)
                    if t == 3 and (g := at(5)):
                        act.wait_ge(lg_done, g.index + 1)
                        nc.scalar.activation(logit_rows[:], lg_ps[0:E, :], ACT.Identity, bias=br_col[:, 0:1]
                                             ).then_inc(lg_copied, 1)
                    if g := at(2):
                        act.wait_ge(hid_done, TPG * g.index + t + 1)
                        nc.scalar.activation(hidden[:, t], hid_ps[:, t], ACT.Square, scale=H1 ** -0.5,
                                             accum_out=sumsq[:, g.parity, t:t + 1]).then_inc(sumsq_ready, 1)
                    if t == 0 and (g := at(3)):
                        for u in range(2, TPG):
                            silu(g, u)
                    if t == 0 and (g := at(6)):
                        act.wait_ge(lg_turned, g.index + 1)
                        if g.after(1):
                            act.wait_ge(chosen_ready, g.index)
                        nc.scalar.activation(logits[:].rearrange("p t e -> p (t e)"), lg_ps[:, 0:TPG * E], ACT.Copy
                                             ).then_inc(logits_ready, 1)
                    if t == 2 and (g := at(1)):
                        act.wait_ge(agg_done, g.index + 1)
                        if g.after(2):
                            act.wait_ge(hid_done, TPG * (g.index - 1))
                        nc.scalar.activation(agg[:, g.parity], agg_ps, ACT.Copy).then_inc(agg_copied, 1)
                    if t == 3 and (g := at(4)):
                        act.wait_ge(tok_turned, g.index + 1)
                        if g.after(2):
                            act.wait_ge(x2_stored[g.parity], 16 * g.half)
                            act.wait_ge(xn2_ready, g.index - 1)
                        nc.scalar.activation(x2[:, g.parity], tok_ps, ACT.Copy).then_inc(x2_kept, 1)
                if g := at(6):
                    if g.after(2) and not g.late:
                        act.wait_ge(rows_sent[g.parity], 16 * 2 * TPG * g.half)
                    nc.scalar.activation(rows_out[:, g.rows, :, 0:D], xn2[:, g.parity], ACT.Copy
                                         ).then_inc(rows_copied, 1)
                if g := at(2):
                    for t in range(2):
                        silu(g, t)

            act.wait_ge(consts_in, CONSTS)
            steps(act, step)

            def tile_step(at, quad, q, second=False):
                if tile := at(0):
                    number, turn, k = tile
                    act.wait_ge(xt_turned, number + 1)
                    nc.scalar.activation(xg_t[:, k % 2], xt_ps[:, k % 2, 0:P], ACT.Identity,
                                         bias=beta_col[:, 0:1], scale=gamma_col[:, 0:1]).then_inc(xg_t_ready, 1)
                if tile := at(GELU_LAG):
                    number, turn, k = tile
                    act.wait_ge(h_biased, number + 1)
                    nc.scalar.activation(hidden_e[:, k % 4], hidden_e[:, k % 4], ACT.Gelu).then_inc(gelu_done, 1)
                if tile := at(TURN_LAG):
                    number, turn, k = tile
                    act.wait_ge(ht_turned, number + 1)
                    nc.scalar.activation(hidden_et[:, k % 2], ht_ps[:, k % 2, 0:HE], ACT.Copy).then_inc(ht_copied, 1)

            tile_steps(act, tile_step)

        @block.vector
        def _(dve):
            def prep():
                nc.vector.memset(fillers[:, :, 0:D + 2], 0.0)
                nc.vector.memset(expert_f[:], 0.0)
                nc.vector.memset(ones_bf[:], 1.0)
                nc.vector.memset(chosen[:], 0.0)
                nc.vector.memset(bias_sel[:].bitcast(F32), 0.0)
                nc.vector.memset(bias_parts[:].bitcast(F32), 0.0).then_inc(fills_done, 1)
                dve.wait_ge(fills_done, 1)
                for r in (0, 32):
                    nc.vector.memset(bias_sel[r:r + 1, :].bitcast(F32), 1.0)
                dve.wait_ge(fixed_in_sbuf, 32)
                nc.vector.tensor_copy(ends[:, 0], region)
                nc.vector.tensor_copy(target[:], token)
                nc.vector.tensor_copy(fillers[:, :, D + 2].bitcast(U32), unused).then_inc(fillers_ready, 1)
                nc.vector.tensor_copy(before_bf[:], before).then_inc(rank_consts, 1)
                nc.vector.tensor_scalar(eps_ident[:], ident, eps_col[:, 0:1], None, ALU.mult
                                        ).then_inc(fills_done, 1)
                dve.wait_ge(fills_done, 2)

            def prep_bias():
                dve.wait_ge(consts_in, CONSTS)
                nc.vector.tensor_copy(bias_parts[0:1, :], bias_raw[0:1, :])
                nc.vector.tensor_copy(bias_hi[32:33, :], bias_raw[32:33, :]).then_inc(fills_done, 1)
                dve.wait_ge(fills_done, 3)
                nc.vector.tensor_tensor(bias_parts[32:33, :], bias_raw[32:33, :], bias_hi[32:33, :].bitcast(F32),
                                        ALU.subtract).then_inc(bias_ready, 1)

            def residual(g):
                dve.wait_ge(z_done, g.index + 1)
                dve.wait_ge(xf_in[g.parity], 16 * (g.half + 1))
                x_g = x_feat[:, g.parity]
                nc.vector.scalar_tensor_tensor(x_g, z_ps, gb2_col[:, 0:1], x_g, ALU.add, ALU.add
                                               ).then_inc(x2_ready, 1)

            def expert_input(g):
                dve.wait_ge(feat_turned, g.index + 1)
                if g.after(2):
                    dve.wait_ge(lg_done, g.index - 1)
                nc.vector.tensor_scalar(xg[:, g.parity], feat_ps, gamma_col[:, 0:1], beta_col[:, 0:1],
                                        ALU.mult, ALU.add).then_inc(xg_ready, 1)

            def add_epsilon(g):
                dve.wait_ge(adj_in[g.parity], 16 * (g.half + 1))
                for c in range(2):
                    blocks = adj[:, g.parity].rearrange("p (b c) n -> p b c n", c=2)[:, :, c, c * P:(c + 1) * P]
                    last = nc.vector.tensor_tensor(blocks, blocks, eps_ident[:].unsqueeze(1).to_broadcast([P, 2, P]),
                                                   ALU.add)
                last.then_inc(adj_ready, 1)

            def stats1(g):
                dve.wait_ge(x_in[g.parity], 16 * (g.half + 1))
                for t in range(TPG):
                    last = nc.vector.bn_stats(bn1[:, t], x_tok[:, g.parity, t])
                last.then_inc(bn1_done, 1)

            def gather1(g):
                for t in range(TPG):
                    last = nc.vector.bn_aggr(mv1[:, g.parity, t], bn1[:, t])
                last.then_inc(stats1_ready, 1)

            def variance1(g):
                dve.wait_ge(stats1_ready, g.index + 1)
                nc.vector.tensor_scalar(var1[:], mv1[:, g.parity, :, 1], LN_EPS, None, ALU.add
                                        ).then_inc(var1_ready, 1)

            def normalise1(g):
                dve.wait_ge(rstd1_ready, g.index + 1)
                if g.after(2):
                    dve.wait_ge(agg_done, g.index - 1)
                for t in range(TPG):
                    last = nc.vector.tensor_scalar(xn1[:, g.parity, t], x_tok[:, g.parity, t],
                                                   mv1[:, g.parity, t, 0:1], rstd1[:, g.parity, t:t + 1],
                                                   ALU.subtract, ALU.mult)
                last.then_inc(xn1_ready, 1)

            def rms_scale(g, t):
                if t == 0:
                    dve.wait_ge(rrms_ready, g.index + 1)
                nc.vector.scalar_tensor_tensor(hidden[:, t], hid_ps[:, t], rrms[:, g.parity, t:t + 1],
                                               rms_bc[:], ALU.mult, ALU.mult).then_inc(normed, 1)

            def stats2(g):
                dve.wait_ge(x2_kept, g.index + 1)
                for t in range(TPG):
                    last = nc.vector.bn_stats(bn2[:, t], x2[:, g.parity, t * P:(t + 1) * P])
                last.then_inc(bn2_done, 1)

            def gather2(g):
                for t in range(TPG):
                    last = nc.vector.bn_aggr(mv2[:, g.parity, t], bn2[:, t])
                last.then_inc(stats2_ready, 1)

            def variance2(g):
                dve.wait_ge(stats2_ready, g.index + 1)
                nc.vector.tensor_scalar(var2[:], mv2[:, g.parity, :, 1], 1.0 + LN_EPS, LN_EPS * LN_EPS,
                                        ALU.mult, ALU.add).then_inc(var2_ready, 1)

            def normalise2(g):
                dve.wait_ge(rstd2_ready, g.index + 1)
                if g.after(2):
                    dve.wait_ge(rows_copied, g.index - 1)
                for t in range(TPG):
                    last = nc.vector.tensor_scalar(xn2[:, g.parity, t],
                                                   x2[:, g.parity, t * P:(t + 1) * P],
                                                   mv2[:, g.parity, t, 0:1], rstd2[:, g.parity, t:t + 1],
                                                   ALU.subtract, ALU.mult)
                last.then_inc(xn2_ready, 1)

            def spread(col):
                return col[:].unsqueeze(2).to_broadcast([P, TPG, E])

            def largest(g, n, values, top):
                if n:
                    dve.wait_ge(round_link, ROUND * g.index + n)
                nc.vector.tensor_reduce(top[:], values[:], AX.X, ALU.max).then_inc(round_link, 1)

            def where_equal(g, n, values, top, out, link=round_link):
                dve.wait_ge(round_link, ROUND * g.index + n)
                nc.vector.tensor_tensor(out, values, spread(top), ALU.is_equal).then_inc(link, 1)

            def weigh(g, n):
                dve.wait_ge(round_link, ROUND * g.index + n)
                nc.vector.tensor_tensor(score[:], score[:], falling, ALU.mult).then_inc(round_link, 1)

            def take_out_first(g, n):
                dve.wait_ge(round_link, ROUND * g.index + n)
                nc.vector.scalar_tensor_tensor(masked[:], chosen[:, 0:TPG, 0], -3.0e38, logits[:], ALU.mult, ALU.add
                                               ).then_inc(round_link, 1)

            def distance(g):
                dve.wait_ge(round_link, ROUND * g.index + 7)
                nc.vector.tensor_tensor(apart[:], top2[:], top1[:], ALU.subtract).then_inc(apart_ready, 1)

            def shares(g, n):
                if n == 0:
                    dve.wait_ge(power_ready, g.index + 1)
                    nc.vector.tensor_scalar(denom[:], power[:], 1.0, None, ALU.add).then_inc(round_link, 1)
                elif n == 1:
                    dve.wait_ge(round_link, ROUND * g.index + 11)
                    nc.vector.reciprocal(share[:, g.parity, 0], denom[:]).then_inc(round_link, 1)
                else:
                    dve.wait_ge(round_link, ROUND * g.index + 12)
                    nc.vector.tensor_tensor(share[:, g.parity, 1], share[:, g.parity, 0], power[:], ALU.mult
                                            ).then_inc(shares_ready, 1)

            def places(g, n):
                p = g.parity
                if n == 0:
                    dve.wait_ge(ranked_done, g.index + 1)
                    nc.vector.tensor_tensor(rank[:], rank_ps[:, 0:TPG],
                                            ends[:, p].unsqueeze(1).to_broadcast([P, TPG, 2 * E]), ALU.add
                                            ).then_inc(place_link, 1)
                    nc.vector.tensor_tensor(ends[:, 1 - p], ends[:, p], rank_ps[:, TPG], ALU.add
                                            ).then_inc(place_link, 1)
                elif n == 1:
                    dve.wait_ge(place_link, PLACE * g.index + 2)
                    nc.vector.tensor_tensor(ranked[:], chosen[:, 0:TPG].rearrange("p t c e -> p t (c e)"), rank[:],
                                            ALU.mult).then_inc(place_link, 1)
                elif n == 2:
                    dve.wait_ge(place_link, PLACE * g.index + 3)
                    nc.vector.tensor_reduce(row_f[:], ranked[:].rearrange("p t (c e) -> p (t c) e", e=E), AX.X,
                                            ALU.add).then_inc(place_link, 1)
                    dve.wait_ge(shares_ready, g.index + 1)
                    dve.wait_ge(rows_copied, g.index + 1)
                    nc.vector.tensor_copy(rows_out[:, g.rows, :, D:D + 2], share[:, p].rearrange("p c t -> p t c"))
                    nc.vector.tensor_copy(rows_out[:, g.rows, :, D + 2].bitcast(U32), target[:]
                                          ).then_inc(targets_used, 1)
                else:
                    dve.wait_ge(place_link, PLACE * g.index + 4)
                    nc.vector.tensor_copy(row_of[:, g.rows], row_f[:]).then_inc(rows_ready, 1)
                    dve.wait_ge(targets_used, g.index + 1)
                    nc.vector.tensor_scalar(target[:], target[:], float(GT), None, ALU.add).then_inc(place_end, 1)

            def table():
                links = [0]

                def link(ins):
                    links[0] += 1
                    ins.then_inc(table_link, 1)
                    dve.wait_ge(table_link, links[0])

                dve.wait_ge(place_link, PLACE * (NG - 1) + 2)
                nc.vector.tensor_copy(ends_i[:], ends[:, 0]).then_inc(ends_ready, 1)
                rows = padded[:].rearrange("p c e -> p (c e)")
                link(nc.vector.tensor_tensor(rows, ends[:, 0], region, ALU.subtract))
                link(nc.vector.tensor_scalar(count_i[:], rows, float(P - 1), None, ALU.add))
                link(nc.vector.tensor_scalar(count_i[:], count_i[:], 7, 7, ALU.logical_shift_right,
                                             ALU.logical_shift_left))
                link(nc.vector.tensor_copy(rows, count_i[:]))
                for c in range(2):
                    last = nc.vector.tensor_tensor(upto_p[:, c], upto, padded[:, c:c + 1].to_broadcast([P, E, E]),
                                                   ALU.mult)
                nc.vector.tensor_scalar(jump[:], padded[:], -1.0, float(CAP), ALU.mult, ALU.add)
                link(last)
                link(nc.vector.tensor_reduce(upto_rows[:], upto_p[:], AX.X, ALU.add))
                link(nc.vector.tensor_scalar(passed[:], upto_rows[:], tile_row, None, ALU.is_le))
                nc.vector.tensor_reduce(columns[:, 0:2], passed[:], AX.X, ALU.add)
                link(nc.vector.tensor_tensor(jumps[:], passed[:], jump[:], ALU.mult))
                link(nc.vector.tensor_reduce(columns[:, 2:4], jumps[:], AX.X, ALU.add))
                for c in range(2):
                    last = nc.vector.tensor_scalar(columns[:, 2 + c:3 + c], columns[:, 2 + c:3 + c], tile_row,
                                                   float(c * AREA), ALU.add, ALU.add)
                last.then_inc(columns_ready, 1)
                dve.wait_ge(columns_turned, 1)
                nc.vector.tensor_copy(first_row[:].rearrange("p (c i) -> p c i", c=2), column_ps[:, 2:4, 0:HALF]
                                      ).then_inc(table_ready, 1)
                link(nc.vector.tensor_scalar(
                    expert_f[:, LAST_LAG:LAST_LAG + TILES].rearrange("p (c i) -> p c i", c=2),
                    column_ps[:, 0:2, 0:HALF], float(E - 1), None, ALU.min))

                def experts_from(field):
                    return expert_f[:, field:field + (WORDS - 1) * PER_WORD + 1:PER_WORD]

                def joined(out, low, high, fields):
                    return nc.vector.scalar_tensor_tensor(out, high, float(E ** fields), low, ALU.mult, ALU.add)

                for i in range(3):
                    last = joined(two_f[:, i], experts_from(2 * i), experts_from(2 * i + 1), 1)
                link(last)
                joined(four_f[:, 0], two_f[:, 0], two_f[:, 1], 2)
                link(joined(four_f[:, 1], two_f[:, 2], experts_from(FIELDS - 1), 2))
                joined(word[:], four_f[:, 0], four_f[:, 1], 4).then_inc(table_ready, 1)

            def step(at):
                if (g := at(1)) and not g.after(1):
                    prep_bias()
                if g := at(5):
                    normalise2(g)
                if g := at(4):
                    residual(g)
                if g := at(0):
                    stats1(g)
                    dve.wait_ge(bn1_done, g.index + 1)
                if g := at(6):
                    dve.wait_ge(logits_ready, g.index + 1)
                    largest(g, 0, logits, top1)
                if g := at(0):
                    gather1(g)
                if g := at(6):
                    where_equal(g, 1, logits[:], top1, score[:])
                if g := at(0):
                    variance1(g)
                if g := at(6):
                    weigh(g, 2)
                if g := at(0):
                    add_epsilon(g)
                if g := at(6):
                    largest(g, 3, score, place)
                if g := at(5):
                    expert_input(g)
                if g := at(6):
                    where_equal(g, 4, falling, place, chosen[:, 0:TPG, 0])
                    take_out_first(g, 5)
                    largest(g, 6, masked, top2)
                    distance(g)
                    where_equal(g, 7, masked[:], top2, score[:])
                    weigh(g, 8)
                if g := at(0):
                    normalise1(g)
                if g := at(6):
                    largest(g, 9, score, place)
                    where_equal(g, 10, falling, place, chosen[:, 0:TPG, 1], chosen_ready)
                if g := at(6):
                    places(g, 0)
                if g := at(2):
                    rms_scale(g, 0)
                if g := at(4):
                    stats2(g)
                    dve.wait_ge(bn2_done, g.index + 1)
                if g := at(2):
                    rms_scale(g, 1)
                if g := at(4):
                    gather2(g)
                if g := at(4):
                    variance2(g)
                if g := at(2):
                    rms_scale(g, 2)
                if g := at(6):
                    shares(g, 0)
                if g := at(2):
                    rms_scale(g, 3)
                if g := at(6):
                    places(g, 1)
                    shares(g, 1)
                    shares(g, 2)
                    places(g, 2)
                    places(g, 3)
                    if g.late and g.index == NG - 1:
                        table()

            prep()
            steps(dve, step)
            dve.wait_ge(table_ready, 2)

            word_now = [None]

            def tile_step(at, quad, q, second=False):
                if q == 0:
                    word_now[0] = dve.value_load(word[0:1, bass.ds(quad, 1)], min_val=0, max_val=E ** FIELDS - 1)
                first_at, last_at = experts_of(word_now[0], q, D)
                if tile := at(SCALE_LAG):
                    number, _, k = tile
                    dve.wait_ge(y_biased, number + 1)
                    weight = D + int(number >= HALF if isinstance(number, int) else second)
                    nc.vector.tensor_scalar(result[:, k % SENDS], result[:, k % SENDS],
                                            rows_in[:, k, weight:weight + 1], None, ALU.mult).then_inc(result_ready, 1)
                if tile := at(FIRST_LAG):
                    number, turn, k = tile
                    dve.wait_ge(h_done, number + 1)
                    nc.vector.tensor_tensor(hidden_e[:, k % 4], h_ps[:, k % 2, 0:HE],
                                            b1_bc[:, bass.ds(first_at, HE)], ALU.add).then_inc(h_biased, 1)
                if tile := at(LAST_LAG):
                    number, turn, k = tile
                    dve.wait_ge(y_done, number + 1)
                    if later(number, SENDS):
                        dve.wait_ge(result_sent[k % SENDS], 16 * (turn * (RING // SENDS) + k // SENDS))
                    nc.vector.tensor_tensor(result[:, k % SENDS], y_ps[:, k % 2, 0:D], b2_bc[:, bass.ds(last_at, D)],
                                            ALU.add).then_inc(y_biased, 1)

            tile_steps(dve, tile_step)


def kernel(x, adj, L0_gnn_epsilon, L0_gnn_W1, L0_gnn_b1, L0_gnn_rms_weight, L0_gnn_W2, L0_gnn_b2,
           L0_ffn_gamma, L0_ffn_beta, L0_ffn_Wr, L0_ffn_br, L0_ffn_W1, L0_ffn_b1, L0_ffn_W2, L0_ffn_b2):
    import concourse.bacc as bacc
    from concourse.bass_utils import run_bass_kernel_spmd

    x = np.asarray(x)
    arrays = {
        "x": x.reshape(NTOK, D),
        "x_t": x.reshape(NTOK, D).T,
        "adj_t": np.asarray(adj).transpose(0, 2, 1).reshape(NTOK, NODES),
        "eps": np.asarray(L0_gnn_epsilon).reshape(1),
        "gw1": np.asarray(L0_gnn_W1),
        "gb1": np.asarray(L0_gnn_b1).reshape(1, H1),
        "rms_w": np.asarray(L0_gnn_rms_weight),
        "gw2": np.asarray(L0_gnn_W2),
        "gb2": np.asarray(L0_gnn_b2).reshape(D, 1),
        "gamma": np.asarray(L0_ffn_gamma).reshape(D, 1),
        "beta": np.asarray(L0_ffn_beta).reshape(D, 1),
        "wr": np.asarray(L0_ffn_Wr),
        "br": np.asarray(L0_ffn_br).reshape(E, 1),
        "w1": np.asarray(L0_ffn_W1),
        "b1": np.asarray(L0_ffn_b1).reshape(E * HE),
        "w2": np.asarray(L0_ffn_W2),
        "b2": np.asarray(L0_ffn_b2).reshape(E * D),
        "fixed_in": constants()[0],
    }
    arrays = {k: np.ascontiguousarray(v) for k, v in arrays.items()}
    nc = bacc.Bacc("TRN2", target_bir_lowering=False, num_devices=1)
    args = [nc.dram_tensor(k, v.shape, mybir.dt.from_np(v.dtype), kind="ExternalInput").ap()
            for k, v in arrays.items()]
    out = nc.dram_tensor("out", (NTOK + 2 * E * P, D), F32, kind="ExternalOutput").ap()
    build(nc, *args, out)
    result = run_bass_kernel_spmd(nc, [arrays], core_ids=[0])
    return np.ascontiguousarray(result.results[0]["out"][:NTOK]).reshape(x.shape)
```
